# Optimizing a Trainium2 kernel written in Bass

```python
import numpy as np
import jax
import jax.numpy as jnp

def _softmax(x, axis=-1):
    return jax.nn.softmax(x, axis=axis)

def _gelu(x):
    return jax.nn.gelu(x, approximate=True)

def _silu(x):
    return jax.nn.silu(x)

def _sigmoid(x):
    return jax.nn.sigmoid(x)

def _layernorm(x, axis=-1, eps=1e-05):
    m = jnp.mean(x, axis=axis, keepdims=True)
    v = jnp.var(x, axis=axis, keepdims=True)
    return (x - m) / jnp.sqrt(v + eps)

def _scatter_add(tgt, idx, src, axis=0):
    return tgt.at[idx].add(src)

def _segment_sum(src, seg, n):
    return jax.ops.segment_sum(src, seg, n)
kernel_name = 'mk_adaln_d1_jaxref_r4_ea7bb2'

def setup_inputs(seed: int=0):
    np.random.seed(seed)
    _w = jnp.asarray

    def _L0_attn_setup():
        import jax, jax.numpy as jnp
        import numpy as np
        DIM = 1024
        NUM_HEAD = 32
        NUM_KV_HEAD = 8
        ROPE_THETA = 10000.0
        B, T = (2, 512)

        def apply_rope(x, start_pos=0, theta=ROPE_THETA):
            d = x.shape[-1]
            half = d // 2
            inv_freq = 1.0 / theta ** (jnp.arange(0, half, dtype=jnp.float32) / half)
            pos = jnp.arange(x.shape[1], dtype=jnp.float32) + start_pos
            ang = pos[:, None] * inv_freq[None, :]
            cos = jnp.cos(ang)[None, :, None, :]
            sin = jnp.sin(ang)[None, :, None, :]
            x1, x2 = (x[..., :half], x[..., half:])
            return jnp.concatenate([x1 * cos - x2 * sin, x1 * sin + x2 * cos], axis=-1)
        key = jax.random.key(seed)
        ks = jax.random.split(key, 5)
        scale = 0.02
        X = jax.random.normal(ks[0], (B, T, DIM), dtype=jnp.float32)
        Wq = jax.random.normal(ks[1], (DIM, DIM), dtype=jnp.float32) * scale
        Wk = jax.random.normal(ks[2], (DIM, DIM // NUM_HEAD * NUM_KV_HEAD), dtype=jnp.float32) * scale
        Wv = jax.random.normal(ks[3], (DIM, DIM // NUM_HEAD * NUM_KV_HEAD), dtype=jnp.float32) * scale
        Wo = jax.random.normal(ks[4], (DIM, DIM), dtype=jnp.float32) * scale
        return {'X': X, 'Wq': Wq, 'Wk': Wk, 'Wv': Wv, 'Wo': Wo}
    _L0_attn_in = _L0_attn_setup()

    def _L0_ffn_setup():
        import jax, jax.numpy as jnp
        import numpy as np
        RANKS = (8, 16, 32, 64)
        TOPK = 1
        SCALING = 1.0 / 4
        key = jax.random.key(seed)
        ks = jax.random.split(key, 7)
        D_IN, D_OUT, MAX_R, N_RANKS = (1024, 1024, 64, len(RANKS))
        B_, S_ = (4, 512)
        return {'hidden_states': jax.random.normal(ks[0], (B_, S_, D_IN), jnp.float32), 'W': jax.random.normal(ks[1], (D_OUT, D_IN), jnp.float32) * 0.02, 'b': jax.random.normal(ks[2], (D_OUT,), jnp.float32) * 0.02, 'A': jax.random.normal(ks[3], (MAX_R, D_IN), jnp.float32) * 0.02, 'B': jnp.zeros((D_OUT, MAX_R), jnp.float32) + jax.random.normal(ks[4], (D_OUT, MAX_R), jnp.float32) * 0.02, 'gate_w': jax.random.normal(ks[5], (N_RANKS, D_IN), jnp.float32) * 0.02, 'gate_b': jax.random.normal(ks[6], (N_RANKS,), jnp.float32) * 0.02}
    _L0_ffn_in = _L0_ffn_setup()
    _L0_c = _w((lambda *s: np.random.randn(*s).astype(np.float32) * 0.05)(2, 1024))
    _L0_wmod = _w((lambda *s: np.random.randn(*s).astype(np.float32) * 0.05)(1024, 6 * 1024) * 1024 ** (-0.5))
    _d = {'L0_attn_X': _L0_attn_in['X'], 'L0_attn_Wq': _L0_attn_in['Wq'], 'L0_attn_Wk': _L0_attn_in['Wk'], 'L0_attn_Wv': _L0_attn_in['Wv'], 'L0_attn_Wo': _L0_attn_in['Wo'], 'L0_ffn_W': _L0_ffn_in['W'], 'L0_ffn_b': _L0_ffn_in['b'], 'L0_ffn_A': _L0_ffn_in['A'], 'L0_ffn_B': _L0_ffn_in['B'], 'L0_ffn_gate_w': _L0_ffn_in['gate_w'], 'L0_ffn_gate_b': _L0_ffn_in['gate_b'], 'L0_c': _L0_c, 'L0_wmod': _L0_wmod}
    _x0 = _d['L0_attn_X']
    _d['L0_attn_X'] = jax.random.normal(jax.random.fold_in(jax.random.key(seed), 1), (2, 2048, 1024), dtype=_x0.dtype)
    del _x0
    return _d

def reference(L0_attn_X, L0_attn_Wq, L0_attn_Wk, L0_attn_Wv, L0_attn_Wo, L0_ffn_W, L0_ffn_b, L0_ffn_A, L0_ffn_B, L0_ffn_gate_w, L0_ffn_gate_b, L0_c, L0_wmod):

    def _L0_attn_ref(X, Wq, Wk, Wv, Wo):
        import jax, jax.numpy as jnp
        import numpy as np
        DIM = 1024
        NUM_HEAD = 32
        NUM_KV_HEAD = 8
        ROPE_THETA = 10000.0
        B, T = (2, 512)

        def apply_rope(x, start_pos=0, theta=ROPE_THETA):
            d = x.shape[-1]
            half = d // 2
            inv_freq = 1.0 / theta ** (jnp.arange(0, half, dtype=jnp.float32) / half)
            pos = jnp.arange(x.shape[1], dtype=jnp.float32) + start_pos
            ang = pos[:, None] * inv_freq[None, :]
            cos = jnp.cos(ang)[None, :, None, :]
            sin = jnp.sin(ang)[None, :, None, :]
            x1, x2 = (x[..., :half], x[..., half:])
            return jnp.concatenate([x1 * cos - x2 * sin, x1 * sin + x2 * cos], axis=-1)
        Bs, Ts, C = X.shape
        H, Hkv = (NUM_HEAD, NUM_KV_HEAD)
        dh = C // H
        G = H // Hkv
        Q = apply_rope((X @ Wq).reshape(Bs, Ts, H, dh))
        K = apply_rope((X @ Wk).reshape(Bs, Ts, Hkv, dh))
        V = (X @ Wv).reshape(Bs, Ts, Hkv, dh)
        Qh = Q.transpose(0, 2, 1, 3).reshape(Bs, Hkv, G, Ts, dh)
        Kh = K.transpose(0, 2, 1, 3)
        Vh = V.transpose(0, 2, 1, 3)
        scores = jnp.einsum('bkgtd,bksd->bkgts', Qh, Kh) / jnp.sqrt(jnp.float32(dh))
        causal = jnp.tril(jnp.ones((Ts, Ts), dtype=bool))
        scores = jnp.where(causal[None, None, None], scores, -jnp.inf)
        attn = jax.nn.softmax(scores, axis=-1)
        out = jnp.einsum('bkgts,bksd->bkgtd', attn, Vh)
        out = out.reshape(Bs, H, Ts, dh).transpose(0, 2, 1, 3).reshape(Bs, Ts, C)
        return out @ Wo

    def _L0_ffn_ref(hidden_states, W, b, A, B, gate_w, gate_b):
        import jax, jax.numpy as jnp
        import numpy as np
        RANKS = (8, 16, 32, 64)
        TOPK = 1
        SCALING = 1.0 / 4
        bsz, seq, d_in = hidden_states.shape
        out = jnp.einsum('bsd,od->bso', hidden_states, W) + b
        x = hidden_states.reshape(-1, d_in)
        scores = x @ gate_w.T + gate_b
        probs = jax.nn.softmax(scores, axis=-1)
        routing_weights, selected = jax.lax.top_k(probs, TOPK)
        routing_weights = routing_weights / jnp.sum(routing_weights, axis=-1, keepdims=True)
        lora_outputs = jnp.stack([x @ A[:r, :].T @ B[:, :r].T for r in RANKS], axis=1)
        sel = jnp.take_along_axis(lora_outputs, selected[:, :, None], axis=1)
        final = jnp.sum(sel * routing_weights[:, :, None], axis=1)
        return out + final.reshape(bsz, seq, -1)
    x = L0_attn_X
    mod = (_silu(L0_c) @ L0_wmod).reshape(L0_c.shape[0], 6, 1, -1)
    sa, ca, ga, sb, cb, gb = (mod[:, 0], mod[:, 1], mod[:, 2], mod[:, 3], mod[:, 4], mod[:, 5])
    ga = (2 * (ga >= 0) - 1) * jnp.maximum(jnp.abs(ga), 0.25)
    gb = (2 * (gb >= 0) - 1) * jnp.maximum(jnp.abs(gb), 0.25)
    h = _layernorm(x, axis=-1) * (1 + ca) + sa
    x = x + ga * _L0_attn_ref(h, L0_attn_Wq, L0_attn_Wk, L0_attn_Wv, L0_attn_Wo)
    h = _layernorm(x, axis=-1) * (1 + cb) + sb
    x = x + gb * _L0_ffn_ref(h, L0_ffn_W, L0_ffn_b, L0_ffn_A, L0_ffn_B, L0_ffn_gate_w, L0_ffn_gate_b)
    return x

_drawn_inputs = setup_inputs


def setup_inputs(seed=0):
    import zlib

    import numpy as np

    out = dict(_drawn_inputs(seed))
    spreads = {}
    factors = {'L0_attn_Wq': 8.0,
     'L0_attn_Wk': 8.0,
     'L0_attn_Wv': 8.0,
     'L0_attn_Wo': 8.0,
     'L0_ffn_b': 64.0,
     'L0_ffn_A': 3.264,
     'L0_ffn_B': 3.253,
     'L0_ffn_gate_w': 15.208,
     'L0_ffn_gate_b': 64.0}
    for name, (base, spread) in spreads.items():
        noise = np.random.default_rng([zlib.crc32(name.encode()), seed]).standard_normal(out[name].shape)
        drawn = base * np.exp(spread * noise) if base else spread * noise
        out[name] = jnp.asarray(drawn.astype(out[name].dtype))
    for name, factor in factors.items():
        out[name] = (out[name] * factor).astype(out[name].dtype)
    return out
```

```python
from contextlib import ExitStack

import numpy as np

import concourse.bass as bass
from concourse import mybir

F32 = mybir.dt.float32
F32R = mybir.dt.float32r
BF16 = mybir.dt.bfloat16
ALU = mybir.AluOpType
ACT = mybir.ActivationFunctionType
AX = mybir.AxisListType

P = 128
B, T, C = 2, 2048, 1024
H, HKV, D = 32, 8, 32
G = H // HKV
KB = C // P
CH = 512
NCH = T // CH
TT = CH // P
NT = T // P
KV = HKV * D
NG = B * HKV
RANKS = (8, 16, 32, 64)
RMAX = RANKS[-1]
NR = len(RANKS)
XW = RMAX + NR
EPS = 1e-5
MASKED = -1e30
SCALE = float(D) ** -0.5
SWAP = [(i + D // 2) % D for i in range(D)]

MOD_COLS = 256
PIECE = KB * MOD_COLS
MOD_BLKS = MOD_COLS // P


def wait_alone(eng, sem, value, met):
    if not isinstance(value, int):
        value = eng.to_reg(value)
    eng.wait_ge(*met)
    eng.wait_ge(sem, value)


def f32(ap):
    return ap.bitcast(F32)


def rows(ap, k=KB):
    return ap.rearrange("(k p) n -> p k n", p=P)


def project(nc, io, scratch, mod):
    QS, KS, VS, GATES = scratch["q"], scratch["k"], scratch["v"], scratch["gates"]
    NSTAGE = 3
    first_mod = 2 * C // MOD_COLS
    in_loop = (6 * C // MOD_COLS - first_mod) // (B * NCH)
    QB, KVB = C // P, KV // P
    UNITS = QB + KVB + TT
    RU = QB + KVB
    with ExitStack() as ctx:
        def sb(name, shape, dt=F32):
            return ctx.enter_context(nc.sbuf_tensor(name, shape, dt))

        def sem(name):
            return ctx.enter_context(nc.semaphore(name))

        stage = sb("stage", [P, NSTAGE, PIECE])
        wq = sb("wq", [P, 2, KB, C], F32R)
        wk = sb("wk", [P, 2, KB, KV], F32R)
        wv = sb("wv", [P, 2, KB, KV], F32R)
        ident = sb("ident_f", [P, P])
        c_t = sb("c_t", [P, KB, B])
        e_c = sb("e_c", [P, KB, B])
        silu = sb("silu", [P, KB, B])
        x = sb("x", [P, TT, C])
        stats = sb("stats", [P, TT, 2, 6])
        mv = sb("mv", [P, TT, 2])
        var = sb("var", [P, TT])
        rstd = sb("rstd", [P, TT])
        minus_half = sb("minus_half", [P, TT])
        hf = sb("hf", [P, 2, CH])
        hT = sb("hT", [P, 2, KB, CH], F32R)
        rope = sb("rope", [P, 2, CH])
        swp = sb("swp", [P, CH])
        xsin = sb("xsin", [P, CH])
        xcos = sb("xcos", [P, CH])
        q = sb("q", [P, 2, CH])
        qhl = sb("qhl", [P, 2, 2, CH], F32R)
        vt = sb("vt", [P, 2, KV])
        acc = ctx.enter_context(nc.psum_tensor("acc", [P, 4, CH], F32))
        tp = ctx.enter_context(nc.psum_tensor("tp", [P, 2, CH], F32))
        mod_ps = ctx.enter_context(nc.psum_tensor("mod_ps", [P, CH], F32))

        consts_in = sem("consts_in")
        stage_in = [sem(f"stage_in{b}") for b in range(NSTAGE)]
        whi_done = sem("whi_done")
        wlo_done = sem("wlo_done")
        c_exp = sem("c_exp")
        silu_done = sem("silu_done")
        mod_mm = sem("mod_mm")
        mod_out = sem("mod_out")
        mod_final = sem("mod_final")
        gates_out = sem("gates_out")
        x_in = sem("x_in")
        rope_in = sem("rope_in")
        var_done = sem("var_done")
        rstd_done = sem("rstd_done")
        xhat_done = sem("xhat_done")
        tp_done = sem("tp_done")
        h_hi = sem("h_hi")
        h_lo = sem("h_lo")
        acc_done = sem("acc_done")
        acc_free = sem("acc_free")
        q_done = sem("q_done")
        q_hi = sem("q_hi")
        q_lo = sem("q_lo")
        q_stored = [sem(f"q_stored{b}") for b in range(2)]
        v_stored = [sem(f"v_stored{b}") for b in range(2)]
        dve_step = sem("dve_step")
        ident_zero = sem("ident_zero")
        ident_done = sem("ident_done")

        wmod = rows(io["wmod"])
        pieces = [(wmod[:, :, m * MOD_COLS:(m + 1) * MOD_COLS], None) for m in range(first_mod)]
        kq = PIECE // C
        for k0 in range(0, KB, kq):
            pieces.append((rows(io["wq"])[:, k0:k0 + kq, :], (wq, k0, kq)))
        pieces.append((rows(io["wk"]), (wk, 0, KB)))
        pieces.append((rows(io["wv"]), (wv, 0, KB)))
        NP = len(pieces)
        NW = NP - first_mod

        def uses(b, before=NP):
            return len(range(b, before, NSTAGE))

        def staged(pi):
            b = pi % NSTAGE
            return stage[:, b, :], b, uses(b, pi) + 1

        with nc.Block() as block:
            @block.sync
            def _(sp):
                sp.dma_start(c_t[:, :, :], io["cT"].rearrange("(k p) b -> p k b", p=P)).then_inc(consts_in, 16)
                for s in (*q_stored, *v_stored):
                    sp.sem_inc(s, 16)

                def load_x(n):
                    sp.dma_start(x[:, :, :], io["x"][bass.ds(n * CH, CH), :].rearrange("(a p) c -> p a c", p=P)).then_inc(x_in, 16)

                load_x(0)
                for pi, (src, _) in enumerate(pieces):
                    buf, b, n = staged(pi)
                    if pi >= NSTAGE:
                        before = pi - NSTAGE
                        if before < first_mod:
                            sp.wait_ge(mod_mm, before + 1)
                        else:
                            sp.wait_ge(wlo_done, before - first_mod + 1)
                    sp.dma_start(buf.rearrange("p (k n) -> p k n", n=src.shape[-1]), src).then_inc(stage_in[b], 16)
                sp.wait_ge(wlo_done, NW)

                def chunk(n, last):
                    bi, j = n // NCH, n % NCH

                    def wait(semaphore, value):
                        wait_alone(sp, semaphore, value, (wlo_done, NW))

                    wait(q_done, n * RU + 1)
                    sp.dma_start(rope[:, :, :], io["rope"][:, :, bass.ds(n * CH, CH)]).then_inc(rope_in, 16)
                    for u in range(in_loop):
                        wait(mod_mm, n * in_loop + (first_mod - in_loop + u + 1))
                        sp.dma_start(stage[:, u, :].rearrange("p (k n) -> p k n", n=MOD_COLS),
                                     wmod[:, :, bass.ds((n * in_loop + (first_mod + u)) * MOD_COLS, MOD_COLS)]).then_inc(stage_in[u], 16)
                    if not last:
                        wait(tp_done, n * KB + (KB + 1))
                        load_x(n + 1)
                    for m in range(RU):
                        wait(q_lo, n * RU + (m + 3))
                        if m < QB:
                            dst = QS[:, bass.ds(bi * C + m * P, P), bass.ds(j * CH, CH)]
                        else:
                            dst = KS[:, bass.ds(bi * KV + (m - QB) * P, P), bass.ds(j * CH, CH)]
                        sp.dma_start(dst.rearrange("s r t -> r s t"), f32(qhl[:, m % 2, :, :])).then_inc(q_stored[m % 2], 16)
                    for a in range(TT):
                        wait(acc_free, n * UNITS + (RU + a + 2))
                        sp.dma_start(VS[bass.ds(bi * HKV, HKV), :, bass.ds(j * TT + a, 1), :].rearrange("g p a d -> p g (a d)"),
                                     vt[:, a % 2, :].rearrange("p (g d) -> p g d", d=D)).then_inc(v_stored[a % 2], 16)

                with sp.Fori(0, B * NCH - 1) as n:
                    chunk(n, False)
                chunk(B * NCH - 1, True)
                sp.wait_ge(mod_final, 3)
                for gi, first in enumerate((2 * KB, 5 * KB)):
                    for b in range(B):
                        sp.dma_start(GATES[b, gi, :].rearrange("(k p) -> p k", p=P),
                                     mod[:, first:first + KB, b], allow_slow_non_contiguous=True).then_inc(gates_out, 16)
                sp.wait_ge(gates_out, 16 * 2 * B)
                for s in q_stored:
                    sp.wait_ge(s, 16 * (B * NCH * RU // 2 + 1))
                for s in v_stored:
                    sp.wait_ge(s, 16 * (B * NCH * TT // 2 + 1))

            @block.gpsimd
            def _(pool):
                nc.gpsimd.memset(ident[:, :], 0.0).then_inc(ident_zero, 1)
                nc.gpsimd.memset(minus_half[:, :], -0.5).then_inc(ident_zero, 1)
                pool.wait_ge(ident_zero, 2)
                nc.gpsimd.affine_select(out=ident[:, :], in_=ident[:, :], compare_op=ALU.not_equal, fill=1.0,
                                        base=0, pattern=[[-1, P]], channel_multiplier=1).then_inc(ident_done, 1)
                pool.sem_inc(q_lo, 2)
                with pool.Fori(0, B * NCH) as n:
                    pool.wait_ge(var_done, n + 1)
                    nc.gpsimd.tensor_tensor(rstd[:, :], var[:, :], minus_half[:, :], ALU.pow).then_inc(rstd_done, 1)
                    for m in range(RU):
                        pool.wait_ge(q_hi, n * RU + (m + 1))
                        pool.wait_ge(q_stored[m % 2], (n * (RU // 2) + (m // 2 + 1)) * 16)
                        nc.gpsimd.tensor_tensor(qhl[:, m % 2, 1, :], q[:, m % 2, :], f32(qhl[:, m % 2, 0, :]),
                                                ALU.subtract).then_inc(q_lo, 1)

            @block.scalar
            def _(act):
                act.wait_ge(consts_in, 16)
                nc.scalar.activation(e_c[:, :, :], c_t[:, :, :], ACT.Exp, scale=-1.0).then_inc(c_exp, 1)
                for pi, (src, w) in enumerate(pieces):
                    if w:
                        buf, b, cnt = staged(pi)
                        act.wait_ge(stage_in[b], 16 * cnt)
                        nc.scalar.activation(w[0][:, 0, w[1]:w[1] + w[2], :], buf.rearrange("p (k n) -> p k n", n=src.shape[-1]),
                                             ACT.Copy).then_inc(whi_done, 1)
                with act.Fori(0, B) as bi:
                    with act.Fori(0, NCH) as j:
                        n = bi * NCH + j
                        act.wait_ge(acc_done, n * UNITS + 1)
                        for k in range(KB):
                            if k >= 2:
                                act.wait_ge(h_lo, n * KB + (k - 1))
                            wait_alone(act, tp_done, n * KB + (k + 2), (mod_out, first_mod))
                            shift, scale = (mod[:, v * KB + k, bass.ds(bi, 1)] for v in (0, 1))
                            nc.scalar.activation(hf[:, k % 2, :], tp[:, k % 2, :], ACT.Identity, bias=shift, scale=scale)
                            nc.scalar.activation(hT[:, 0, k, :], tp[:, k % 2, :], ACT.Identity, bias=shift, scale=scale).then_inc(h_hi, 1)
                        for m in range(RU):
                            act.wait_ge(q_done, n * RU + (m + 2))
                            act.wait_ge(q_stored[m % 2], (n * (RU // 2) + (m // 2 + 1)) * 16)
                            nc.scalar.activation(qhl[:, m % 2, 0, :], q[:, m % 2, :], ACT.Copy).then_inc(q_hi, 1)

            @block.vector
            def _(dve):
                dve.sem_inc(acc_free, 1)
                dve.sem_inc(q_done, 1)
                dve.wait_ge(c_exp, 1)
                nc.vector.tensor_scalar(e_c[:, :, :], e_c[:, :, :], 1.0, None, ALU.add).then_inc(dve_step, 1)
                dve.wait_ge(dve_step, 1)
                nc.vector.reciprocal(silu[:, :, :], e_c[:, :, :]).then_inc(dve_step, 1)
                dve.wait_ge(dve_step, 2)
                nc.vector.tensor_tensor(silu[:, :, :], silu[:, :, :], c_t[:, :, :], ALU.mult).then_inc(silu_done, 1)
                for pi in range(first_mod):
                    dve.wait_ge(mod_mm, pi + 1)
                    src = mod_ps[:, 0:MOD_BLKS * B].rearrange("p (m b) -> p m b", b=B)
                    dst = mod[:, pi * MOD_BLKS:(pi + 1) * MOD_BLKS, :]
                    one = 1.0 if pi * MOD_COLS >= C else 0.0
                    nc.vector.tensor_scalar(dst, src, one, None, ALU.add).then_inc(mod_out, 1)
                wn = 0
                for pi, (src, w) in enumerate(pieces):
                    if w:
                        wn += 1
                        buf, b, _ = staged(pi)
                        v = buf.rearrange("p (k n) -> p k n", n=src.shape[-1])
                        dve.wait_ge(whi_done, wn)
                        nc.vector.tensor_tensor(w[0][:, 1, w[1]:w[1] + w[2], :], v, f32(w[0][:, 0, w[1]:w[1] + w[2], :]),
                                                ALU.subtract).then_inc(wlo_done, 1)
                STEPS = 2 + 2 * RU
                with dve.Fori(0, B * NCH) as n:
                    step = 2
                    dve.wait_ge(x_in, n * 16 + 16)
                    for a in range(TT):
                        for half in range(2):
                            ins = nc.vector.bn_stats(stats[:, a, half, :], x[:, a, half * CH:(half + 1) * CH])
                    ins.then_inc(dve_step, 1)
                    step += 1
                    wait_alone(dve, dve_step, n * STEPS + step, (silu_done, 1))
                    for a in range(TT):
                        ins = nc.vector.bn_aggr(mv[:, a, :], stats[:, a, :, :].rearrange("p h s -> p (h s)"))
                    ins.then_inc(dve_step, 1)
                    step += 1
                    dve.wait_ge(dve_step, n * STEPS + step)
                    nc.vector.tensor_scalar(var[:, :], mv[:, :, 1], EPS, None, ALU.add).then_inc(var_done, 1)
                    dve.wait_ge(rstd_done, n + 1)
                    for a in range(TT):
                        nc.vector.tensor_scalar(x[:, a, :], x[:, a, :], mv[:, a, 0:1], rstd[:, a:a + 1],
                                                ALU.subtract, ALU.mult).then_inc(xhat_done, 1)
                    for k in range(KB):
                        dve.wait_ge(h_hi, n * KB + (k + 1))
                        nc.vector.tensor_tensor(hT[:, 1, k, :], hf[:, k % 2, :], f32(hT[:, 0, k, :]), ALU.subtract).then_inc(h_lo, 1)
                    dve.wait_ge(rope_in, n * 16 + 16)
                    for m in range(RU):
                        dve.wait_ge(q_done, n * RU + (m + 1))
                        wait_alone(dve, acc_done, n * UNITS + (m + 2), (silu_done, 1))
                        nc.vector.stream_shuffle(swp[:, :], acc[:, m % 4, :], SWAP).then_inc(dve_step, 1)
                        nc.vector.tensor_tensor(xcos[:, :], acc[:, m % 4, :], rope[:, 0, :], ALU.mult).then_inc(acc_free, 1)
                        step += 1
                        dve.wait_ge(dve_step, n * STEPS + step)
                        nc.vector.tensor_tensor(xsin[:, :], swp[:, :], rope[:, 1, :], ALU.mult).then_inc(dve_step, 1)
                        step += 1
                        dve.wait_ge(dve_step, n * STEPS + step)
                        dve.wait_ge(acc_free, n * UNITS + (m + 2))
                        dve.wait_ge(q_lo, n * RU + (m + 1))
                        nc.vector.tensor_tensor(q[:, m % 2, :], xcos[:, :], xsin[:, :], ALU.add).then_inc(q_done, 1)
                    for a in range(TT):
                        u = RU + a
                        dve.wait_ge(acc_done, n * UNITS + (u + 2))
                        dve.wait_ge(v_stored[a % 2], (n * (TT // 2) + (a // 2 + 1)) * 16)
                        nc.vector.tensor_copy(vt[:, a % 2, :], acc[:, u % 4, 0:KV]).then_inc(acc_free, 1)
                    for u in range(in_loop):
                        dve.wait_ge(mod_mm, n * in_loop + (first_mod + u + 1))
                        src = mod_ps[:, 0:MOD_BLKS * B].rearrange("p (m b) -> p m b", b=B)
                        nc.vector.tensor_copy(mod[:, bass.ds((n * in_loop + (first_mod + u)) * MOD_BLKS, MOD_BLKS), :], src).then_inc(mod_out, 1)
                dve.wait_ge(mod_out, 6 * C // MOD_COLS)
                step = B * NCH * STEPS + 2
                for first in (2 * KB, 5 * KB):
                    g = mod[:, first:first + KB, :]
                    nc.vector.tensor_scalar(e_c[:, :, :], g, 0.0, 2.0, ALU.is_ge, ALU.mult).then_inc(dve_step, 1)
                    nc.vector.scalar_tensor_tensor(out=c_t[:, :, :], in0=g, scalar=-1.0, in1=g, op0=ALU.mult, op1=ALU.max).then_inc(dve_step, 1)
                    step += 2
                    dve.wait_ge(dve_step, step)
                    nc.vector.tensor_scalar(c_t[:, :, :], c_t[:, :, :], 0.25, None, ALU.max).then_inc(dve_step, 1)
                    step += 1
                    dve.wait_ge(dve_step, step)
                    nc.vector.scalar_tensor_tensor(out=g, in0=e_c[:, :, :], scalar=-1.0, in1=c_t[:, :, :],
                                                   op0=ALU.add, op1=ALU.mult).then_inc(mod_final, 1)
                    dve.wait_ge(mod_final, 1)
                s2 = mod[:, 4 * KB:5 * KB, :]
                nc.vector.tensor_scalar(s2, s2, 1.0, None, ALU.add).then_inc(mod_final, 1)

            @block.tensor
            def _(pe):
                def mod_piece(buf, b, landed, done):
                    pe.wait_ge(stage_in[b], landed)
                    if not isinstance(done, int) or done:
                        pe.wait_ge(mod_out, done)
                    w = buf.rearrange("p (k n) -> p k n", n=MOD_COLS)
                    for m in range(MOD_BLKS):
                        for k in range(KB):
                            ins = nc.tensor.matmul(mod_ps[:, m * B:(m + 1) * B], w[:, k, m * P:(m + 1) * P], silu[:, k, :],
                                                   start=k == 0, stop=k == KB - 1)
                    ins.then_inc(mod_mm, 1)

                pe.sem_inc(acc_done, 1)
                pe.sem_inc(tp_done, 1)
                pe.wait_ge(silu_done, 1)
                pe.wait_ge(ident_done, 1)
                for pi in range(first_mod):
                    buf, b, cnt = staged(pi)
                    mod_piece(buf, b, 16 * cnt, pi)
                with pe.Fori(0, B * NCH) as n:
                    for k in range(KB):
                        if k >= 2:
                            pe.wait_ge(h_hi, n * KB + (k - 1))
                        for a in range(TT):
                            if k == 0:
                                pe.wait_ge(xhat_done, n * TT + (a + 1))
                            ins = nc.tensor.transpose(tp[:, k % 2, a * P:(a + 1) * P], x[:, a, k * P:(k + 1) * P], ident[:, :])
                        ins.then_inc(tp_done, 1)
                    pe.wait_ge(wlo_done, NW)
                    for m in range(RU):
                        w, c0 = (wq, m * P) if m < QB else (wk, (m - QB) * P)
                        pe.wait_ge(acc_free, n * UNITS + max(m - 2, 1))
                        for k in range(KB):
                            if m == 0:
                                pe.wait_ge(h_lo, n * KB + (k + 1))
                            for ws, hs in ((0, 0), (0, 1), (1, 0)):
                                ins = nc.tensor.matmul(acc[:, m % 4, :], w[:, ws, k, c0:c0 + P], hT[:, hs, k, :],
                                                       start=(k, ws, hs) == (0, 0, 0), stop=(k, ws) == (KB - 1, 1))
                        ins.then_inc(acc_done, 1)
                    for a in range(TT):
                        u = RU + a
                        pe.wait_ge(acc_free, n * UNITS + (u - 2))
                        for k in range(KB):
                            for hs, ws in ((0, 0), (0, 1), (1, 0)):
                                ins = nc.tensor.matmul(acc[:, u % 4, 0:KV], hT[:, hs, k, a * P:(a + 1) * P], wv[:, ws, k, :],
                                                       start=(k, ws, hs) == (0, 0, 0), stop=(k, hs) == (KB - 1, 1))
                        ins.then_inc(acc_done, 1)
                    for u in range(in_loop):
                        mod_piece(stage[:, u, :], u, n * 16 + 16 * (uses(u) + 1), n * in_loop + (first_mod + u))


LEAD = 18
MAX_PER_STEP = G
STEPS = [(j, k) for j in range(NCH) for k in range(TT * (j + 1))]
NS = len(STEPS)
MAXIMA = [(j, r, s, h) for j in range(NCH) for r in range(TT) for s in range(j + 1) for h in range(G)]
NM = len(MAXIMA)
assert NM == MAX_PER_STEP * NS


def step_plan(s, last):
    ahead, t = divmod(s + LEAD, NS)
    units = [] if ahead and last else [(ahead, MAX_PER_STEP * t + u) for u in range(MAX_PER_STEP)]
    due = shift_due(ahead, t)
    return units, None if last and due and due[0] else due


def shift_due(ahead, t):
    if t == 0:
        return (ahead - 1, NCH - 1)
    j = STEPS[t][0]
    return (ahead, j - 1) if STEPS[t - 1][0] != j else None


def attend(nc, io, scratch):
    QS, KS, VS, OS = (scratch[k] for k in ("q", "k", "v", "o"))
    PB = 4
    with ExitStack() as ctx:
        def sb(name, shape, dt=F32):
            return ctx.enter_context(nc.sbuf_tensor(name, shape, dt))

        def sem(name):
            return ctx.enter_context(nc.semaphore(name))

        qst = [sb(f"qst{i}", [P, G, T], F32R) for i in range(2)]
        kst = [sb(f"kst{i}", [P, T], F32R) for i in range(2)]
        v = [sb(f"v{i}", [P, NT, D]) for i in range(2)]
        ones = sb("ones", [P, D])
        probs = sb("probs", [P, PB, G, CH])
        ident = sb("ident_a", [P, P])
        ident_b = sb("ident_b", [P, P], BF16)
        mask_q = sb("mask_q", [P, P], BF16)
        mask_k = sb("mask_k", [P, P], BF16)
        maxp = sb("maxp", [P, 2, TT, G, NCH])
        shift = sb("shift", [P, TT, G])
        shift2 = sb("shift2", [P, TT, P], F32R)
        rden = sb("rden", [P, CH])
        o = sb("o", [P, 2, CH])
        ohl = sb("ohl", [P, 2, 2, CH], F32R)
        s_max = ctx.enter_context(nc.psum_tensor("s_max", [P, 2, CH], F32))
        s_exp = [ctx.enter_context(nc.psum_tensor(f"s_exp{i}", [P, 2, CH], F32)) for i in range(2)]
        o_ps = ctx.enter_context(nc.psum_tensor("o_ps", [P, CH], F32))
        den_ps = ctx.enter_context(nc.psum_tensor("den_ps", [P, CH], F32))

        const_set = sem("const_set")
        const_done = sem("const_done")
        ones_done = sem("ones_done")
        loaded = [sem(f"loaded{i}") for i in range(2)]
        max_scores = sem("max_scores")
        max_taken = sem("max_taken")
        shift_step = sem("shift_step")
        shift_ready = sem("shift_ready")
        shift_turned = sem("shift_turned")
        shift_in_act = sem("shift_in_act")
        shift_in_dve = sem("shift_in_dve")
        exp_scores = sem("exp_scores")
        exp_done = sem("exp_done")
        pv_done = sem("pv_done")
        den_read = sem("den_read")
        o_done = sem("o_done")
        o_hi = sem("o_hi")
        o_lo = sem("o_lo")
        o_stored = [sem(f"o_stored{i}") for i in range(2)]
        NLOAD = 7

        def group_pairs(eng, body):
            with eng.Fori(0, NG // 2 - 1) as i:
                for par in range(2):
                    body(i * 2 + par, par, False)
            for par in range(2):
                body(NG - 2 + par, par, par == 1)

        with nc.Block() as block:
            @block.sync
            def _(sp):
                def load(g, par):
                    for row, part in ((0, 0), (1, 1), (2, 0)):
                        sp.dma_start(f32(qst[par][row * D:(row + 1) * D, :, :]),
                                     QS[part, bass.ds(g * P, P), :].rearrange("(h d) t -> d h t", d=D)).then_inc(loaded[par], 16)
                    for row, part in ((0, 0), (1, 0), (2, 1)):
                        sp.dma_start(f32(kst[par][row * D:(row + 1) * D, :]), KS[part, bass.ds(g * D, D), :]).then_inc(loaded[par], 16)
                    sp.dma_start(v[par][:, :, :], VS[bass.ds(g, 1), :, :, :].rearrange("g p a d -> p (g a) d")).then_inc(loaded[par], 16)

                def body(g, par, last):
                    for j in range(NCH):
                        wait_alone(sp, o_lo, g * NCH + (j + 3), (const_set, 4))
                        sp.dma_start(OS[:, bass.ds(g * P, P), j * CH:(j + 1) * CH].rearrange("s r t -> r s t"),
                                     f32(ohl[:, j % 2, :, :])).then_inc(o_stored[j % 2], 16)
                    if not isinstance(g, int):
                        wait_alone(sp, pv_done, g * NS + (NS + PB), (const_set, 4))
                        load(g + 2, par)

                for s in o_stored:
                    sp.sem_inc(s, 16)
                for par in range(2):
                    load(par, par)
                group_pairs(sp, body)
                for s in o_stored:
                    sp.wait_ge(s, 16 * (NG * NCH // 2 + 1))

            @block.gpsimd
            def _(pool):
                for t, fill in ((ident[:, :], 0.0), (ident_b[:, :], 0.0), (mask_q[:, :], 0.0), (mask_k[:, :], 0.0)):
                    nc.gpsimd.memset(t, fill).then_inc(const_set, 1)
                nc.gpsimd.memset(ones[:, :], 1.0).then_inc(const_done, 1)
                nc.gpsimd.memset(f32(shift2[:, :, :]), 0.0).then_inc(const_done, 1)
                pool.wait_ge(const_set, 4)
                for t in (ident, ident_b):
                    nc.gpsimd.affine_select(out=t[:, :], in_=t[:, :], compare_op=ALU.not_equal, fill=1.0,
                                            base=0, pattern=[[-1, P]], channel_multiplier=1).then_inc(const_done, 1)
                nc.gpsimd.affine_select(out=mask_q[:, :], in_=mask_q[:, :], compare_op=ALU.is_ge, fill=MASKED,
                                        base=0, pattern=[[-1, P]], channel_multiplier=1).then_inc(const_done, 1)
                nc.gpsimd.affine_select(out=mask_k[:, :], in_=mask_k[:, :], compare_op=ALU.is_ge, fill=MASKED,
                                        base=0, pattern=[[1, P]], channel_multiplier=-1).then_inc(const_done, 1)

                def body(g, par, last):
                    for j in range(NCH):
                        b = j % 2
                        wait_alone(pool, o_done, g * NCH + (j + 2), (const_set, 4))
                        wait_alone(pool, o_stored[b], (g * (NCH // 2) + (j // 2 + 1)) * 16, (const_set, 4))
                        nc.gpsimd.tensor_copy(ohl[:, b, 0, :], o[:, b, :]).then_inc(o_hi, 1)
                        pool.wait_ge(o_hi, g * NCH + (j + 1))
                        nc.gpsimd.tensor_tensor(ohl[:, b, 1, :], o[:, b, :], f32(ohl[:, b, 0, :]), ALU.subtract).then_inc(o_lo, 1)

                pool.sem_inc(o_lo, 2)
                group_pairs(pool, body)

            def turned_shift(eng_copy, eng, done, g, par, j, heads):
                eng.wait_ge(shift_turned, g * NCH + (j + 1))
                for h in heads:
                    ins = eng_copy(qst[par][3 * D:3 * D + 2, h, j * CH:(j + 1) * CH], s_max[h * D:h * D + 2, 1, :])
                ins.then_inc(done, 1)

            @block.scalar
            def _(act):
                def copy(dst, src):
                    return nc.scalar.activation(dst, src, ACT.Copy)

                def body(g, par, last):
                    for s, (j, k) in enumerate(STEPS):
                        c0 = max(k - TT * j, 0) * P
                        _, due = step_plan(s, last)
                        for p in range(2):
                            act.wait_ge(exp_scores, g * (2 * NS) + (2 * s + p + 1))
                            if p == 0:
                                act.wait_ge(pv_done, g * NS + (s + 1))
                            nc.scalar.activation(probs[:, s % PB, 2 * p:2 * p + 2, c0:CH], s_exp[p][:, :, c0:CH], ACT.Exp,
                                                 scale=SCALE).then_inc(exp_done, 1)
                            if p == 0 and due:
                                turned_shift(copy, act, shift_in_act, g + due[0], (par + due[0]) % 2, due[1], (0, 1))

                act.sem_inc(exp_done, 2)
                for t in range(1, LEAD):
                    if due := shift_due(0, t):
                        turned_shift(copy, act, shift_in_act, 0, 0, due[1], (0, 1))
                group_pairs(act, body)

            @block.vector
            def _(dve):
                def maximum(g, m):
                    j, r, s, h = MAXIMA[m]
                    n = CH if s < j else (r + 1) * P
                    dve.wait_ge(max_scores, g * NM + (m + 1))
                    nc.vector.tensor_reduce(maxp[:, j % 2, r, h, s:s + 1], s_max[:, m % 2, 0:n], AX.X, ALU.max).then_inc(max_taken, 1)

                def finish_shift(g, m):
                    j = MAXIMA[m][0]
                    dve.wait_ge(max_taken, g * NM + (m + 1))
                    if not isinstance(g, int) or g * NCH + j:
                        dve.wait_ge(shift_turned, g * NCH + j)
                    nc.vector.tensor_reduce(shift[:, :, :], maxp[:, j % 2, :, :, 0:j + 1], AX.X, ALU.max, negate=True).then_inc(shift_step, 1)
                    dve.wait_ge(shift_step, g * (2 * NCH) + (2 * j + 1))
                    parts = shift2[:, :, :].rearrange("p r (h d) -> p r h d", d=D)
                    nc.vector.tensor_copy(parts[:, :, :, 0], shift[:, :, :]).then_inc(shift_step, 1)
                    dve.wait_ge(shift_step, g * (2 * NCH) + (2 * j + 2))
                    nc.vector.tensor_tensor(parts[:, :, :, 1], shift[:, :, :], f32(parts[:, :, :, 0]), ALU.subtract).then_inc(shift_ready, 1)

                def copy(dst, src):
                    return nc.vector.tensor_copy(dst, src)

                def ahead(g, par, units, due):
                    for i, (a, m) in enumerate(units):
                        if i == 1 and due:
                            turned_shift(copy, dve, shift_in_dve, g + due[0], (par + due[0]) % 2, due[1], (2, 3))
                        maximum(g + a, m)
                        if m == NM - 1 or MAXIMA[m + 1][0] != MAXIMA[m][0]:
                            finish_shift(g + a, m)
                    if due and not units:
                        turned_shift(copy, dve, shift_in_dve, g + due[0], (par + due[0]) % 2, due[1], (2, 3))

                def normalize(g, j):
                    steps_of = sum(TT * (i + 1) for i in range(j + 1))
                    dve.wait_ge(pv_done, g * NS + (steps_of + PB))
                    nc.vector.reciprocal(rden[:, :], den_ps[:, :]).then_inc(den_read, 1)
                    dve.wait_ge(den_read, g * NCH + (j + 1))
                    dve.wait_ge(o_lo, g * NCH + (j + 1))
                    nc.vector.tensor_tensor(o[:, j % 2, :], o_ps[:, :], rden[:, :], ALU.mult).then_inc(o_done, 1)

                def body(g, par, last):
                    for s, (j, k) in enumerate(STEPS):
                        ahead(g, par, *step_plan(s, last))
                        if k == 0 and j:
                            normalize(g, j - 1)
                    normalize(g, NCH - 1)

                for par in range(2):
                    nc.vector.memset(f32(kst[par][3 * D:3 * D + 2, :]), 1.0).then_inc(ones_done, 1)
                dve.sem_inc(o_done, 1)
                dve.wait_ge(const_done, 6)
                for t in range(LEAD):
                    ahead(0, 0, [(0, MAX_PER_STEP * t + u) for u in range(MAX_PER_STEP)], shift_due(0, t) if t else None)
                group_pairs(dve, body)

            @block.tensor
            def _(pe):
                def max_unit(g, par, m):
                    j, r, s, h = MAXIMA[m]
                    n = CH if s < j else (r + 1) * P
                    q0 = j * CH + r * P
                    if not isinstance(g, int) or g * NM + m > 1:
                        pe.wait_ge(max_taken, g * NM + (m - 1))
                    ins = nc.tensor.matmul(s_max[:, m % 2, 0:n], qst[par][0:3 * D, h, q0:q0 + P],
                                           kst[par][0:3 * D, s * CH:s * CH + n], start=True, stop=s < j)
                    if s == j:
                        ins = nc.tensor.matmul(s_max[:, m % 2, n - P:n], ident_b[:, :], mask_q[:, :], start=False, stop=True)
                    ins.then_inc(max_scores, 1)

                def turn_shift(g, j):
                    pe.wait_ge(shift_ready, g * NCH + (j + 1))
                    for r in range(TT):
                        ins = nc.tensor.transpose(s_max[:, 1, r * P:(r + 1) * P], f32(shift2[:, r, :]), ident[:, :])
                    ins.then_inc(shift_turned, 1)

                def shift_read(g, j):
                    pe.wait_ge(shift_in_act, g * NCH + (j + 1))
                    pe.wait_ge(shift_in_dve, g * NCH + (j + 1))

                def pair_scores(g, par, s, p):
                    j, k = STEPS[s]
                    c0 = max(k - TT * j, 0) * P
                    pe.wait_ge(exp_done, g * (2 * NS) + (2 * s + p + 1))
                    for i in range(2):
                        diag = k >= TT * j
                        ins = nc.tensor.matmul(s_exp[p][:, i, c0:CH], kst[par][0:3 * D + 2, k * P:(k + 1) * P],
                                               qst[par][0:3 * D + 2, 2 * p + i, j * CH + c0:(j + 1) * CH], start=True, stop=not diag)
                        if diag:
                            ins = nc.tensor.matmul(s_exp[p][:, i, c0:c0 + P], ident_b[:, :], mask_k[:, :], start=False, stop=True)
                    ins.then_inc(exp_scores, 1)

                def products(g, par, s):
                    j, k = STEPS[s]
                    c0 = max(k - TT * j, 0) * P
                    pe.wait_ge(exp_done, g * (2 * NS) + (2 * s + 4))
                    if k == 0:
                        pe.wait_ge(o_done, g * NCH + (j + 1))
                    for out, w in ((o_ps, v[par][:, k, :]), (den_ps, ones[:, :])):
                        for h in range(G):
                            ins = nc.tensor.matmul(out[h * D:(h + 1) * D, c0:CH], w, probs[:, s % PB, h, c0:CH],
                                                   start=k == 0, stop=k == TT * (j + 1) - 1)
                    ins.then_inc(pv_done, 1)

                def body(g, par, last):
                    for s in range(NS):
                        units, due = step_plan(s, last)
                        if units and units[0] == (1, 0):
                            pe.wait_ge(loaded[1 - par], load_count(g, par))
                        pair_scores(g, par, s, 0)
                        for a, m in units[:1 if due else 2]:
                            max_unit(g + a, (par + a) % 2, m)
                        if due:
                            turn_shift(g + due[0], due[1])
                        pair_scores(g, par, s, 1)
                        if not due:
                            for a, m in units[2:]:
                                max_unit(g + a, (par + a) % 2, m)
                        if s:
                            products(g, par, s - 1)
                        if due:
                            shift_read(g + due[0], due[1])
                            for a, m in units[1:]:
                                max_unit(g + a, (par + a) % 2, m)
                    products(g, par, NS - 1)

                def load_count(g, par):
                    if isinstance(g, int):
                        return 16 * NLOAD * ((g + 1) // 2 + 1)
                    return (g - par) * (8 * NLOAD) + 16 * NLOAD * (1 + par)

                pe.wait_ge(const_done, 6)
                pe.wait_ge(ones_done, 2)
                pe.wait_ge(loaded[0], 16 * NLOAD)
                pe.sem_inc(pv_done, PB)
                for t in range(LEAD):
                    due = shift_due(0, t) if t else None
                    for u in range(MAX_PER_STEP):
                        if due and u == 1:
                            turn_shift(0, due[1])
                            shift_read(0, due[1])
                        max_unit(0, 0, MAX_PER_STEP * t + u)
                group_pairs(pe, body)


def feed(nc, io, scratch, mod, out):
    OS, GATES = scratch["o"], scratch["gates"]
    NSTAGE = 3
    with ExitStack() as ctx:
        def sb(name, shape, dt=F32):
            return ctx.enter_context(nc.sbuf_tensor(name, shape, dt))

        def psum(name, shape):
            return ctx.enter_context(nc.psum_tensor(name, shape, F32))

        def sem(name):
            return ctx.enter_context(nc.semaphore(name))

        wo = sb("wo", [P, 2, KB, C], F32R)
        w = sb("w", [P, 2, KB, C + XW], F32R)
        bb = sb("bb", [RMAX + 1, C])
        gate_b = sb("gate_b", [P, NR])
        gates = sb("gates", [P, 2, C])
        work = sb("work", [P, NSTAGE, C])
        xh, t2, hf = (work[:, i, :] for i in range(3))
        ot = [sb(f"ot{i}", [P, 2, KB, P], F32R) for i in range(2)]
        x = [sb(f"x{i}", [P, C]) for i in range(2)]
        hT = sb("hT2", [P, 2, KB, P], F32R)
        ident = sb("ident_g", [P, P])
        stats = sb("stats2", [P, 2, 6])
        mv = sb("mv2", [P, 2])
        var = sb("var2", [P, 1])
        rstd = sb("rstd2", [P, 1])
        minus_half = sb("minus_half2", [P, 1])
        lg = sb("lg", [P, NR])
        nmax = sb("nmax", [P, 1])
        e = sb("e", [P, NR])
        esum = sb("esum", [P, 1])
        rsum = sb("rsum", [P, 1])
        pr = sb("pr", [P, NR])
        pmax = sb("pmax", [P, 1])
        rpmax = sb("rpmax", [P, 1])
        wt = sb("wt", [P, 1])
        beyond = sb("beyond", [P, NR])
        zm = sb("zm", [P, RMAX + 1])
        zt = sb("zt", [RMAX + 1, P])
        y1 = psum("y1", [P, 2, CH])
        y2 = psum("y2", [P, 2, CH])
        tp = psum("tp2", [P, 2, CH])
        z = psum("z", [P, CH])
        ztp = psum("ztp", [P, CH])

        stage_in = [sem(f"fstage_in{b}") for b in range(NSTAGE)]
        consts_in = sem("fconsts_in")
        ident_zero = sem("fident_zero")
        consts_done = sem("fconsts_done")
        whi_done = sem("fwhi_done")
        wlo_done = sem("fwlo_done")
        gates_in = sem("gates_in")
        ot_in = [sem(f"ot_in{i}") for i in range(2)]
        x_in = [sem(f"fx_in{i}") for i in range(2)]
        y1_done = sem("y1_done")
        y1_read = sem("y1_read")
        step_x = sem("step_x")
        var_done = sem("fvar_done")
        rstd_done = sem("frstd_done")
        xhat_done = sem("fxhat_done")
        tp_done = sem("ftp_done")
        hf_done = sem("hf_done")
        h_hi = sem("fh_hi")
        h_lo = sem("fh_lo")
        z_done = sem("z_done")
        main_done = sem("main_done")
        step_z = sem("step_z")
        lg_done = sem("lg_done")
        e_done = sem("e_done")
        zm_done = sem("zm_done")
        ztp_done = sem("ztp_done")
        zt_done = sem("zt_done")
        y2_done = sem("y2_done")
        t2_done = sem("t2_done")
        out_done = sem("out_done")
        stored = sem("stored")

        pieces = [(rows(io["wo"])[:, k, :], wo[:, :, k, :]) for k in range(KB)]
        pieces += [(rows(io["wT"])[:, k, :], w[:, :, k, 0:C]) for k in range(KB)]
        NP = len(pieces) + 1
        extra = work[:, (NP - 1) % NSTAGE, 0:KB * XW].rearrange("p (k n) -> p k n", n=XW)

        def split_pieces():
            for i in range(NP):
                b = i % NSTAGE
                if i < NP - 1:
                    dst = pieces[i][1]
                    yield work[:, b, :], dst[:, 0, :], dst[:, 1, :], b, i // NSTAGE + 1
                else:
                    yield extra, w[:, 0, :, C:C + XW], w[:, 1, :, C:C + XW], b, i // NSTAGE + 1

        def tiles(eng, body):
            for n in range(2):
                body(n, n)
            with eng.Fori(1, NT // 2 - 1) as i:
                for par in range(2):
                    body(i * 2 + par, par)
            for n in range(NT - 2, NT):
                body(n, n % 2)

        def is_last(n):
            return isinstance(n, int) and n == NT - 1

        def is_first(n):
            return isinstance(n, int) and n == 0

        with nc.Block() as block:
            @block.sync
            def _(sp):
                for i, (src, _) in enumerate(pieces):
                    if i >= NSTAGE:
                        sp.wait_ge(wlo_done, i - NSTAGE + 1)
                    sp.dma_start(work[:, i % NSTAGE, :], src).then_inc(stage_in[i % NSTAGE], 16)
                sp.wait_ge(wlo_done, NP - NSTAGE)
                sp.dma_start(extra[:, :, 0:RMAX], rows(io["aT"])).then_inc(consts_in, 16)
                sp.dma_start(extra[:, :, RMAX:XW], rows(io["gate_wT"])).then_inc(consts_in, 16)
                sp.dma_start(bb[0:RMAX, :], io["bT"]).then_inc(consts_in, 16)
                sp.dma_start(bb[RMAX:RMAX + 1, :], io["b"].rearrange("(a n) -> a n", a=1)).then_inc(consts_in, 16)
                sp.dma_start(gate_b[:, :], io["gate_b"].rearrange("(a n) -> a n", a=1).broadcast_to((P, NR))).then_inc(consts_in, 16)
                sp.sem_inc(stored, 16)

                def load_o(b, n, par):
                    cols = bass.ds(n * P, P)
                    for s in range(2):
                        sp.dma_start(f32(ot[par][:, s, :, :]),
                                     OS[s, bass.ds(b * C, C), cols].rearrange("(k p) t -> p k t", p=P)).then_inc(ot_in[par], 16)

                def load_x(b, n, par):
                    sp.dma_start(x[par][:, :], io["x"][bass.ds(b * T + n * P, P), :]).then_inc(x_in[par], 16)

                def store(b, n, par):
                    wait_alone(sp, out_done, b * NT + (n + 1), (consts_done, 2))
                    sp.dma_start(out[bass.ds(b * T + n * P, P), :], x[par][:, :]).then_inc(stored, 16)
                    wait_alone(sp, stored, (b * NT + n) * 16 + 32, (consts_done, 2))

                with sp.Fori(0, B) as b:
                    for i in range(2):
                        sp.dma_start(gates[:, i, :], GATES[bass.ds(b, 1), i, :].broadcast_to((P, C))).then_inc(gates_in, 16)
                    load_o(b, 0, 0)
                    load_o(b, 1, 1)
                    load_x(b, 0, 0)

                    def body(n, par):
                        if not (isinstance(n, int) and n + 2 >= NT):
                            wait_alone(sp, y1_done, b * NT + (n + 1), (consts_done, 2))
                            load_o(b, n + 2, par)
                        if not is_first(n):
                            store(b, n - 1, 1 - par)
                        if not is_last(n):
                            load_x(b, n + 1, 1 - par)

                    tiles(sp, body)
                    store(b, NT - 1, (NT - 1) % 2)

            @block.gpsimd
            def _(pool):
                nc.gpsimd.memset(ident[:, :], 0.0).then_inc(ident_zero, 1)
                nc.gpsimd.memset(minus_half[:, :], -0.5).then_inc(ident_zero, 1)
                nc.gpsimd.memset(zm[:, RMAX:RMAX + 1], 1.0).then_inc(consts_done, 1)
                pool.wait_ge(ident_zero, 2)
                nc.gpsimd.affine_select(out=ident[:, :], in_=ident[:, :], compare_op=ALU.not_equal, fill=1.0,
                                        base=0, pattern=[[-1, P]], channel_multiplier=1).then_inc(consts_done, 1)

                with pool.Fori(0, B * NT) as n:
                    pool.wait_ge(var_done, n + 1)
                    nc.gpsimd.tensor_tensor(rstd[:, :], var[:, :], minus_half[:, :], ALU.pow).then_inc(rstd_done, 1)

            @block.scalar
            def _(act):
                for i, (src, hi, _, b, cnt) in enumerate(split_pieces()):
                    if i < NP - 1:
                        act.wait_ge(stage_in[b], 16 * cnt)
                    else:
                        act.wait_ge(consts_in, 16 * 5)
                    nc.scalar.activation(hi, src, ACT.Copy).then_inc(whi_done, 1)

                with act.Fori(0, B) as b:
                    def affine(n):
                        if not is_first(n):
                            act.wait_ge(main_done, b * NT + n)
                        wait_alone(act, tp_done, b * NT + (n + 1), (whi_done, NP))
                        for k in range(KB):
                            shift, scale = (mod[:, v * KB + k, bass.ds(b, 1)] for v in (3, 4))
                            ins = nc.scalar.activation(hf[:, k * P:(k + 1) * P], tp[:, k // TT, (k % TT) * P:(k % TT + 1) * P],
                                                       ACT.Identity, bias=shift, scale=scale)
                        ins.then_inc(hf_done, 1)
                        act.wait_ge(hf_done, b * NT + (n + 1))
                        nc.scalar.activation(hT[:, 0, :, :], hf.rearrange("p (k t) -> p k t", t=P), ACT.Copy).then_inc(h_hi, 1)

                    def body(n, par):
                        act.wait_ge(lg_done, b * NT + (n + 1))
                        nc.scalar.activation(e[:, :], lg[:, :], ACT.Exp, bias=nmax[:, :], accum_out=esum[:, :]).then_inc(e_done, 1)
                        act.wait_ge(ztp_done, b * NT + (n + 1))
                        nc.scalar.activation(zt[:, :], ztp[0:RMAX + 1, 0:P], ACT.Copy).then_inc(zt_done, 1)
                        if not is_last(n):
                            affine(n + 1)

                    affine(0)
                    tiles(act, body)

            @block.vector
            def _(dve):
                for i, (src, hi, lo, _, _) in enumerate(split_pieces()):
                    dve.wait_ge(whi_done, i + 1)
                    nc.vector.tensor_tensor(lo, src, f32(hi), ALU.subtract).then_inc(wlo_done, 1)
                dve.wait_ge(wlo_done, NP)
                dve.wait_ge(consts_done, 2)

                with dve.Fori(0, B) as b:
                    dve.wait_ge(gates_in, b * 32 + 32)

                    XS = 4

                    def norm(n, par):
                        def step(ins, i):
                            ins.then_inc(step_x, 1)
                            dve.wait_ge(step_x, (b * NT + n) * XS + (i + 1))

                        dve.wait_ge(y1_done, b * NT + (n + 1))
                        if not is_first(n):
                            dve.wait_ge(tp_done, b * NT + n)
                        dve.wait_ge(x_in[par], (b * NT + n - par) * 8 + 16)
                        step(nc.vector.tensor_tensor(xh, y1[:, :, :].rearrange("p h c -> p (h c)"), gates[:, 0, :], ALU.mult), 0)
                        step(nc.vector.tensor_tensor(x[par][:, :], x[par][:, :], xh, ALU.add), 1)
                        for half in range(2):
                            ins = nc.vector.bn_stats(stats[:, half, :], x[par][:, half * CH:(half + 1) * CH])
                        ins.then_inc(step_x, 1)
                        wait_alone(dve, step_x, (b * NT + n) * XS + 3, (wlo_done, NP))
                        step(nc.vector.bn_aggr(mv[:, :], stats[:, :, :].rearrange("p h s -> p (h s)")), 3)
                        nc.vector.tensor_scalar(var[:, :], mv[:, 1:2], EPS, None, ALU.add).then_inc(var_done, 1)
                        dve.wait_ge(rstd_done, b * NT + (n + 1))
                        nc.vector.tensor_scalar(xh, x[par][:, :], mv[:, 0:1], rstd[:, :], ALU.subtract, ALU.mult).then_inc(xhat_done, 1)

                    def low_part(n):
                        dve.wait_ge(h_hi, b * NT + (n + 1))
                        nc.vector.tensor_tensor(hT[:, 1, :, :], hf.rearrange("p (k t) -> p k t", t=P), f32(hT[:, 0, :, :]),
                                                ALU.subtract).then_inc(h_lo, 1)

                    ZS = 7

                    def route(n):
                        def step(ins, i):
                            ins.then_inc(step_z, 1)
                            dve.wait_ge(step_z, (b * NT + n) * ZS + (i + 1))

                        dve.wait_ge(z_done, b * NT + (n + 1))
                        step(nc.vector.tensor_tensor(lg[:, :], z[:, RMAX:XW], gate_b[:, :], ALU.add), 0)
                        nc.vector.tensor_reduce(nmax[:, :], lg[:, :], AX.X, ALU.max, negate=True).then_inc(lg_done, 1)
                        dve.wait_ge(e_done, b * NT + (n + 1))
                        step(nc.vector.reciprocal(rsum[:, :], esum[:, :]), 1)
                        step(nc.vector.tensor_scalar(pr[:, :], e[:, :], rsum[:, :], None, ALU.mult), 2)
                        step(nc.vector.tensor_reduce(pmax[:, :], pr[:, :], AX.X, ALU.max), 3)
                        nc.vector.reciprocal(rpmax[:, :], pmax[:, :])
                        step(nc.vector.tensor_scalar(beyond[:, :], pr[:, :], pmax[:, :], None, ALU.is_lt), 4)
                        nc.vector.tensor_tensor(wt[:, :], pmax[:, :], rpmax[:, :], ALU.mult)
                        step(nc.vector.tensor_tensor(beyond[:, 1:2], beyond[:, 1:2], beyond[:, 0:1], ALU.mult), 5)
                        step(nc.vector.tensor_tensor(beyond[:, 2:3], beyond[:, 2:3], beyond[:, 1:2], ALU.mult), 6)
                        if not is_first(n):
                            dve.wait_ge(ztp_done, b * NT + n)
                        nc.vector.tensor_scalar(zm[:, 0:RANKS[0]], z[:, 0:RANKS[0]], wt[:, :], None, ALU.mult)
                        for i in range(NR - 1):
                            lo, hi = RANKS[i], RANKS[i + 1]
                            ins = nc.vector.tensor_scalar(zm[:, lo:hi], z[:, lo:hi], wt[:, :], beyond[:, i:i + 1], ALU.mult, ALU.mult)
                        ins.then_inc(zm_done, 1)

                    def finish(n, par):
                        dve.wait_ge(y2_done, b * NT + (n + 1))
                        nc.vector.tensor_tensor(t2, y2[:, :, :].rearrange("p h c -> p (h c)"), gates[:, 1, :], ALU.mult).then_inc(t2_done, 1)
                        dve.wait_ge(t2_done, b * NT + (n + 1))
                        nc.vector.tensor_tensor(x[par][:, :], x[par][:, :], t2, ALU.add).then_inc(out_done, 1)

                    def body(n, par):
                        if not is_last(n):
                            norm(n + 1, 1 - par)
                        route(n)
                        if not is_last(n):
                            low_part(n + 1)
                        finish(n, par)

                    norm(0, 0)
                    low_part(0)
                    tiles(dve, body)

            @block.tensor
            def _(pe):
                pe.wait_ge(wlo_done, NP)
                pe.wait_ge(consts_done, 2)
                with pe.Fori(0, B) as b:
                    def attention_out(n, par):
                        pe.wait_ge(ot_in[par], (b * NT + n - par) * 16 + 32)
                        if not is_first(n):
                            pe.wait_ge(xhat_done, b * NT + n)
                        for c in range(2):
                            for k in range(KB):
                                for o_s, w_s in ((0, 0), (0, 1), (1, 0)):
                                    ins = nc.tensor.matmul(y1[:, c, :], ot[par][:, o_s, k, :], wo[:, w_s, k, c * CH:(c + 1) * CH],
                                                           start=(k, o_s, w_s) == (0, 0, 0), stop=(k, o_s) == (KB - 1, 1))
                        ins.then_inc(y1_done, 1)

                    def turn(n):
                        pe.wait_ge(xhat_done, b * NT + (n + 1))
                        if not is_first(n):
                            pe.wait_ge(hf_done, b * NT + n)
                        for k in range(KB):
                            ins = nc.tensor.transpose(tp[:, k // TT, (k % TT) * P:(k % TT + 1) * P], xh[:, k * P:(k + 1) * P], ident[:, :])
                        ins.then_inc(tp_done, 1)

                    def linear(n):
                        pe.wait_ge(h_lo, b * NT + (n + 1))
                        if not is_first(n):
                            pe.wait_ge(zm_done, b * NT + n)
                        for dst, c0, c1 in ((z[:, 0:XW], C, C + XW), (y2[:, 0, :], 0, CH), (y2[:, 1, :], CH, C)):
                            if c0 == 0 and not is_first(n):
                                pe.wait_ge(t2_done, b * NT + n)
                            for k in range(KB):
                                for hs, ws in ((0, 0), (0, 1), (1, 0)):
                                    ins = nc.tensor.matmul(dst, hT[:, hs, k, :], w[:, ws, k, c0:c1], start=(k, hs, ws) == (0, 0, 0),
                                                           stop=c0 == C and (k, hs) == (KB - 1, 1))
                            if c0 == C:
                                ins.then_inc(z_done, 1)
                        ins.then_inc(main_done, 1)

                    def lora_turn(n):
                        pe.wait_ge(zm_done, b * NT + (n + 1))
                        if not is_first(n):
                            pe.wait_ge(zt_done, b * NT + n)
                        nc.tensor.transpose(ztp[0:RMAX + 1, 0:P], zm[:, :], ident[:, :]).then_inc(ztp_done, 1)

                    def lora(n):
                        pe.wait_ge(zt_done, b * NT + (n + 1))
                        for c in range(2):
                            ins = nc.tensor.matmul(y2[:, c, :], zt[:, :], bb[:, c * CH:(c + 1) * CH], start=False, stop=True)
                        ins.then_inc(y2_done, 1)

                    def body(n, par):
                        if not is_last(n):
                            attention_out(n + 1, 1 - par)
                        linear(n)
                        lora_turn(n)
                        if not is_last(n):
                            turn(n + 1)
                        lora(n)

                    attention_out(0, 0)
                    turn(0)
                    tiles(pe, body)


def build(nc, io, out):
    with ExitStack() as ctx:
        scratch = {
            "q": nc.dram_tensor("q_scratch", (2, B * C, T), F32, kind="Internal").ap(),
            "k": nc.dram_tensor("k_scratch", (2, B * KV, T), F32, kind="Internal").ap(),
            "v": nc.dram_tensor("v_scratch", (NG, P, NT, D), F32, kind="Internal").ap(),
            "o": nc.dram_tensor("o_scratch", (2, B * C, T), F32, kind="Internal").ap(),
            "gates": nc.dram_tensor("gates_scratch", (B, 2, C), F32, kind="Internal").ap(),
        }
        mod = ctx.enter_context(nc.sbuf_tensor("mod", [P, 6 * KB, B], F32))
        project(nc, io, scratch, mod)
        attend(nc, io, scratch)
        feed(nc, io, scratch, mod, out)


def rope_table():
    half = D // 2
    inv_freq = (np.float32(1.0) / np.float32(10000.0) ** (np.arange(half, dtype=np.float32) / np.float32(half))).astype(np.float32)
    ang = inv_freq[:, None] * np.arange(T, dtype=np.float32)[None, :]
    cos, sin = np.cos(ang), np.sin(ang)
    head = np.stack([np.concatenate([cos, cos]), np.concatenate([-sin, sin])], axis=1)
    return np.ascontiguousarray(np.tile(head, (P // D, 1, B)).astype(np.float32))


def kernel(L0_attn_X, L0_attn_Wq, L0_attn_Wk, L0_attn_Wv, L0_attn_Wo, L0_ffn_W, L0_ffn_b, L0_ffn_A, L0_ffn_B,
           L0_ffn_gate_w, L0_ffn_gate_b, L0_c, L0_wmod):
    import concourse.bacc as bacc
    from concourse.bass_utils import run_bass_kernel_spmd

    t = np.ascontiguousarray
    arrays = {
        "x": t(np.asarray(L0_attn_X).reshape(B * T, C)), "wq": t(L0_attn_Wq), "wk": t(L0_attn_Wk), "wv": t(L0_attn_Wv),
        "wo": t(L0_attn_Wo), "wT": t(np.asarray(L0_ffn_W).T), "b": t(L0_ffn_b), "aT": t(np.asarray(L0_ffn_A).T),
        "bT": t(np.asarray(L0_ffn_B).T), "gate_wT": t(np.asarray(L0_ffn_gate_w).T), "gate_b": t(L0_ffn_gate_b),
        "cT": t(np.asarray(L0_c).T), "wmod": t(L0_wmod), "rope": rope_table(),
    }
    nc = bacc.Bacc("TRN2", target_bir_lowering=False, num_devices=1)
    io = {k: nc.dram_tensor(f"in_{k}", a.shape, mybir.dt.from_np(a.dtype), kind="ExternalInput").ap() for k, a in arrays.items()}
    out = nc.dram_tensor("out", (B * T, C), F32, kind="ExternalOutput").ap()
    build(nc, io, out)
    r = run_bass_kernel_spmd(nc, [{f"in_{k}": a for k, a in arrays.items()}], core_ids=[0])
    return r.results[0]["out"].reshape(B, T, C)
```

```python
from contextlib import ExitStack

import numpy as np

import concourse.bass as bass
from concourse import mybir

F32 = mybir.dt.float32
F32R = mybir.dt.float32r
BF16 = mybir.dt.bfloat16
ALU = mybir.AluOpType
ACT = mybir.ActivationFunctionType
AX = mybir.AxisListType

P = 128
B, T, C = 2, 2048, 1024
H, HKV, D = 32, 8, 32
G = H // HKV
KB = C // P
CH = 512
NCH = T // CH
TT = CH // P
NT = T // P
KV = HKV * D
NG = B * HKV
RANKS = (8, 16, 32, 64)
RMAX = RANKS[-1]
NR = len(RANKS)
XW = RMAX + NR
EPS = 1e-5
MASKED = -1e30
SCALE = float(D) ** -0.5
SWAP = [(i + D // 2) % D for i in range(D)]

MOD_COLS = 256
PIECE = KB * MOD_COLS
MOD_BLKS = MOD_COLS // P


def wait_alone(eng, sem, value, met):
    if not isinstance(value, int):
        value = eng.to_reg(value)
    eng.wait_ge(*met)
    eng.wait_ge(sem, value)


def f32(ap):
    return ap.bitcast(F32)


def rows(ap, k=KB):
    return ap.rearrange("(k p) n -> p k n", p=P)


def project(nc, io, scratch, mod):
    QS, KS, VS, GATES = scratch["q"], scratch["k"], scratch["v"], scratch["gates"]
    NSTAGE = 3
    first_mod = 2 * C // MOD_COLS
    in_loop = (6 * C // MOD_COLS - first_mod) // (B * NCH)
    QB, KVB = C // P, KV // P
    UNITS = QB + KVB + TT
    RU = QB + KVB
    with ExitStack() as ctx:
        def sb(name, shape, dt=F32):
            return ctx.enter_context(nc.sbuf_tensor(name, shape, dt))

        def sem(name):
            return ctx.enter_context(nc.semaphore(name))

        stage = sb("stage", [P, NSTAGE, PIECE])
        wq = sb("wq", [P, 2, KB, C], F32R)
        wk = sb("wk", [P, 2, KB, KV], F32R)
        wv = sb("wv", [P, 2, KB, KV], F32R)
        ident = sb("ident_f", [P, P])
        c_t = sb("c_t", [P, KB, B])
        e_c = sb("e_c", [P, KB, B])
        silu = sb("silu", [P, KB, B])
        x = sb("x", [P, TT, C])
        stats = sb("stats", [P, TT, 2, 6])
        mv = sb("mv", [P, TT, 2])
        var = sb("var", [P, TT])
        rstd = sb("rstd", [P, TT])
        minus_half = sb("minus_half", [P, TT])
        hf = sb("hf", [P, 2, CH])
        hT = sb("hT", [P, 2, KB, CH], F32R)
        rope = sb("rope", [P, 2, CH])
        swp = sb("swp", [P, CH])
        xsin = sb("xsin", [P, CH])
        xcos = sb("xcos", [P, CH])
        q = sb("q", [P, 2, CH])
        qhl = sb("qhl", [P, 2, 2, CH], F32R)
        vt = sb("vt", [P, 2, KV])
        acc = ctx.enter_context(nc.psum_tensor("acc", [P, 4, CH], F32))
        tp = ctx.enter_context(nc.psum_tensor("tp", [P, 2, CH], F32))
        mod_ps = ctx.enter_context(nc.psum_tensor("mod_ps", [P, CH], F32))

        consts_in = sem("consts_in")
        stage_in = [sem(f"stage_in{b}") for b in range(NSTAGE)]
        whi_done = sem("whi_done")
        wlo_done = sem("wlo_done")
        c_exp = sem("c_exp")
        silu_done = sem("silu_done")
        mod_mm = sem("mod_mm")
        mod_out = sem("mod_out")
        mod_final = sem("mod_final")
        gates_out = sem("gates_out")
        x_in = sem("x_in")
        rope_in = sem("rope_in")
        var_done = sem("var_done")
        rstd_done = sem("rstd_done")
        xhat_done = sem("xhat_done")
        tp_done = sem("tp_done")
        h_hi = sem("h_hi")
        h_lo = sem("h_lo")
        acc_done = sem("acc_done")
        acc_free = sem("acc_free")
        q_done = sem("q_done")
        q_hi = sem("q_hi")
        q_lo = sem("q_lo")
        q_stored = [sem(f"q_stored{b}") for b in range(2)]
        v_stored = [sem(f"v_stored{b}") for b in range(2)]
        dve_step = sem("dve_step")
        ident_zero = sem("ident_zero")
        ident_done = sem("ident_done")

        wmod = rows(io["wmod"])
        pieces = [(wmod[:, :, m * MOD_COLS:(m + 1) * MOD_COLS], None) for m in range(first_mod)]
        kq = PIECE // C
        for k0 in range(0, KB, kq):
            pieces.append((rows(io["wq"])[:, k0:k0 + kq, :], (wq, k0, kq)))
        pieces.append((rows(io["wk"]), (wk, 0, KB)))
        pieces.append((rows(io["wv"]), (wv, 0, KB)))
        NP = len(pieces)
        NW = NP - first_mod

        def uses(b, before=NP):
            return len(range(b, before, NSTAGE))

        def staged(pi):
            b = pi % NSTAGE
            return stage[:, b, :], b, uses(b, pi) + 1

        with nc.Block() as block:
            @block.sync
            def _(sp):
                sp.dma_start(c_t[:, :, :], io["cT"].rearrange("(k p) b -> p k b", p=P)).then_inc(consts_in, 16)
                for s in (*q_stored, *v_stored):
                    sp.sem_inc(s, 16)

                def load_x(n):
                    sp.dma_start(x[:, :, :], io["x"][bass.ds(n * CH, CH), :].rearrange("(a p) c -> p a c", p=P)).then_inc(x_in, 16)

                load_x(0)
                for pi, (src, _) in enumerate(pieces):
                    buf, b, n = staged(pi)
                    if pi >= NSTAGE:
                        before = pi - NSTAGE
                        if before < first_mod:
                            sp.wait_ge(mod_mm, before + 1)
                        else:
                            sp.wait_ge(wlo_done, before - first_mod + 1)
                    sp.dma_start(buf.rearrange("p (k n) -> p k n", n=src.shape[-1]), src).then_inc(stage_in[b], 16)
                sp.wait_ge(wlo_done, NW)

                def chunk(n, last):
                    bi, j = n // NCH, n % NCH

                    def wait(semaphore, value):
                        wait_alone(sp, semaphore, value, (wlo_done, NW))

                    wait(q_done, n * RU + 1)
                    sp.dma_start(rope[:, :, :], io["rope"][:, :, bass.ds(n * CH, CH)]).then_inc(rope_in, 16)
                    for u in range(in_loop):
                        wait(mod_mm, n * in_loop + (first_mod - in_loop + u + 1))
                        sp.dma_start(stage[:, u, :].rearrange("p (k n) -> p k n", n=MOD_COLS),
                                     wmod[:, :, bass.ds((n * in_loop + (first_mod + u)) * MOD_COLS, MOD_COLS)]).then_inc(stage_in[u], 16)
                    if not last:
                        wait(tp_done, n * KB + (KB + 1))
                        load_x(n + 1)
                    for m in range(RU):
                        wait(q_lo, n * RU + (m + 3))
                        if m < QB:
                            dst = QS[:, bass.ds(bi * C + m * P, P), bass.ds(j * CH, CH)]
                        else:
                            dst = KS[:, bass.ds(bi * KV + (m - QB) * P, P), bass.ds(j * CH, CH)]
                        sp.dma_start(dst.rearrange("s r t -> r s t"), f32(qhl[:, m % 2, :, :])).then_inc(q_stored[m % 2], 16)
                    for a in range(TT):
                        wait(acc_free, n * UNITS + (RU + a + 2))
                        sp.dma_start(VS[bass.ds(bi * HKV, HKV), :, bass.ds(j * TT + a, 1), :].rearrange("g p a d -> p g (a d)"),
                                     vt[:, a % 2, :].rearrange("p (g d) -> p g d", d=D)).then_inc(v_stored[a % 2], 16)

                with sp.Fori(0, B * NCH - 1) as n:
                    chunk(n, False)
                chunk(B * NCH - 1, True)
                sp.wait_ge(mod_final, 3)
                for gi, first in enumerate((2 * KB, 5 * KB)):
                    for b in range(B):
                        sp.dma_start(GATES[b, gi, :].rearrange("(k p) -> p k", p=P),
                                     mod[:, first:first + KB, b], allow_slow_non_contiguous=True).then_inc(gates_out, 16)
                sp.wait_ge(gates_out, 16 * 2 * B)
                for s in q_stored:
                    sp.wait_ge(s, 16 * (B * NCH * RU // 2 + 1))
                for s in v_stored:
                    sp.wait_ge(s, 16 * (B * NCH * TT // 2 + 1))

            @block.gpsimd
            def _(pool):
                nc.gpsimd.memset(ident[:, :], 0.0).then_inc(ident_zero, 1)
                nc.gpsimd.memset(minus_half[:, :], -0.5).then_inc(ident_zero, 1)
                pool.wait_ge(ident_zero, 2)
                nc.gpsimd.affine_select(out=ident[:, :], in_=ident[:, :], compare_op=ALU.not_equal, fill=1.0,
                                        base=0, pattern=[[-1, P]], channel_multiplier=1).then_inc(ident_done, 1)
                pool.sem_inc(q_lo, 2)
                with pool.Fori(0, B * NCH) as n:
                    pool.wait_ge(var_done, n + 1)
                    nc.gpsimd.tensor_tensor(rstd[:, :], var[:, :], minus_half[:, :], ALU.pow).then_inc(rstd_done, 1)
                    for m in range(RU):
                        pool.wait_ge(q_hi, n * RU + (m + 1))
                        pool.wait_ge(q_stored[m % 2], (n * (RU // 2) + (m // 2 + 1)) * 16)
                        nc.gpsimd.tensor_tensor(qhl[:, m % 2, 1, :], q[:, m % 2, :], f32(qhl[:, m % 2, 0, :]),
                                                ALU.subtract).then_inc(q_lo, 1)

            @block.scalar
            def _(act):
                act.wait_ge(consts_in, 16)
                nc.scalar.activation(e_c[:, :, :], c_t[:, :, :], ACT.Exp, scale=-1.0).then_inc(c_exp, 1)
                for pi, (src, w) in enumerate(pieces):
                    if w:
                        buf, b, cnt = staged(pi)
                        act.wait_ge(stage_in[b], 16 * cnt)
                        nc.scalar.activation(w[0][:, 0, w[1]:w[1] + w[2], :], buf.rearrange("p (k n) -> p k n", n=src.shape[-1]),
                                             ACT.Copy).then_inc(whi_done, 1)
                with act.Fori(0, B) as bi:
                    with act.Fori(0, NCH) as j:
                        n = bi * NCH + j
                        act.wait_ge(acc_done, n * UNITS + 1)
                        for k in range(KB):
                            if k >= 2:
                                act.wait_ge(h_lo, n * KB + (k - 1))
                            wait_alone(act, tp_done, n * KB + (k + 2), (mod_out, first_mod))
                            shift, scale = (mod[:, v * KB + k, bass.ds(bi, 1)] for v in (0, 1))
                            nc.scalar.activation(hf[:, k % 2, :], tp[:, k % 2, :], ACT.Identity, bias=shift, scale=scale)
                            nc.scalar.activation(hT[:, 0, k, :], tp[:, k % 2, :], ACT.Identity, bias=shift, scale=scale).then_inc(h_hi, 1)
                        for m in range(RU):
                            act.wait_ge(q_done, n * RU + (m + 2))
                            act.wait_ge(q_stored[m % 2], (n * (RU // 2) + (m // 2 + 1)) * 16)
                            nc.scalar.activation(qhl[:, m % 2, 0, :], q[:, m % 2, :], ACT.Copy).then_inc(q_hi, 1)

            @block.vector
            def _(dve):
                dve.sem_inc(acc_free, 1)
                dve.sem_inc(q_done, 1)
                dve.wait_ge(c_exp, 1)
                nc.vector.tensor_scalar(e_c[:, :, :], e_c[:, :, :], 1.0, None, ALU.add).then_inc(dve_step, 1)
                dve.wait_ge(dve_step, 1)
                nc.vector.reciprocal(silu[:, :, :], e_c[:, :, :]).then_inc(dve_step, 1)
                dve.wait_ge(dve_step, 2)
                nc.vector.tensor_tensor(silu[:, :, :], silu[:, :, :], c_t[:, :, :], ALU.mult).then_inc(silu_done, 1)
                for pi in range(first_mod):
                    dve.wait_ge(mod_mm, pi + 1)
                    src = mod_ps[:, 0:MOD_BLKS * B].rearrange("p (m b) -> p m b", b=B)
                    dst = mod[:, pi * MOD_BLKS:(pi + 1) * MOD_BLKS, :]
                    one = 1.0 if pi * MOD_COLS >= C else 0.0
                    nc.vector.tensor_scalar(dst, src, one, None, ALU.add).then_inc(mod_out, 1)
                wn = 0
                for pi, (src, w) in enumerate(pieces):
                    if w:
                        wn += 1
                        buf, b, _ = staged(pi)
                        v = buf.rearrange("p (k n) -> p k n", n=src.shape[-1])
                        dve.wait_ge(whi_done, wn)
                        nc.vector.tensor_tensor(w[0][:, 1, w[1]:w[1] + w[2], :], v, f32(w[0][:, 0, w[1]:w[1] + w[2], :]),
                                                ALU.subtract).then_inc(wlo_done, 1)
                STEPS = 2 + 2 * RU
                with dve.Fori(0, B * NCH) as n:
                    step = 2
                    dve.wait_ge(x_in, n * 16 + 16)
                    for a in range(TT):
                        for half in range(2):
                            ins = nc.vector.bn_stats(stats[:, a, half, :], x[:, a, half * CH:(half + 1) * CH])
                    ins.then_inc(dve_step, 1)
                    step += 1
                    wait_alone(dve, dve_step, n * STEPS + step, (silu_done, 1))
                    for a in range(TT):
                        ins = nc.vector.bn_aggr(mv[:, a, :], stats[:, a, :, :].rearrange("p h s -> p (h s)"))
                    ins.then_inc(dve_step, 1)
                    step += 1
                    dve.wait_ge(dve_step, n * STEPS + step)
                    nc.vector.tensor_scalar(var[:, :], mv[:, :, 1], EPS, None, ALU.add).then_inc(var_done, 1)
                    dve.wait_ge(rstd_done, n + 1)
                    for a in range(TT):
                        nc.vector.tensor_scalar(x[:, a, :], x[:, a, :], mv[:, a, 0:1], rstd[:, a:a + 1],
                                                ALU.subtract, ALU.mult).then_inc(xhat_done, 1)
                    for k in range(KB):
                        dve.wait_ge(h_hi, n * KB + (k + 1))
                        nc.vector.tensor_tensor(hT[:, 1, k, :], hf[:, k % 2, :], f32(hT[:, 0, k, :]), ALU.subtract).then_inc(h_lo, 1)
                    dve.wait_ge(rope_in, n * 16 + 16)
                    for m in range(RU):
                        dve.wait_ge(q_done, n * RU + (m + 1))
                        wait_alone(dve, acc_done, n * UNITS + (m + 2), (silu_done, 1))
                        nc.vector.stream_shuffle(swp[:, :], acc[:, m % 4, :], SWAP).then_inc(dve_step, 1)
                        nc.vector.tensor_tensor(xcos[:, :], acc[:, m % 4, :], rope[:, 0, :], ALU.mult).then_inc(acc_free, 1)
                        step += 1
                        dve.wait_ge(dve_step, n * STEPS + step)
                        nc.vector.tensor_tensor(xsin[:, :], swp[:, :], rope[:, 1, :], ALU.mult).then_inc(dve_step, 1)
                        step += 1
                        dve.wait_ge(dve_step, n * STEPS + step)
                        dve.wait_ge(acc_free, n * UNITS + (m + 2))
                        dve.wait_ge(q_lo, n * RU + (m + 1))
                        nc.vector.tensor_tensor(q[:, m % 2, :], xcos[:, :], xsin[:, :], ALU.add).then_inc(q_done, 1)
                    for a in range(TT):
                        u = RU + a
                        dve.wait_ge(acc_done, n * UNITS + (u + 2))
                        dve.wait_ge(v_stored[a % 2], (n * (TT // 2) + (a // 2 + 1)) * 16)
                        nc.vector.tensor_copy(vt[:, a % 2, :], acc[:, u % 4, 0:KV]).then_inc(acc_free, 1)
                    for u in range(in_loop):
                        dve.wait_ge(mod_mm, n * in_loop + (first_mod + u + 1))
                        src = mod_ps[:, 0:MOD_BLKS * B].rearrange("p (m b) -> p m b", b=B)
                        nc.vector.tensor_copy(mod[:, bass.ds((n * in_loop + (first_mod + u)) * MOD_BLKS, MOD_BLKS), :], src).then_inc(mod_out, 1)
                dve.wait_ge(mod_out, 6 * C // MOD_COLS)
                step = B * NCH * STEPS + 2
                for first in (2 * KB, 5 * KB):
                    g = mod[:, first:first + KB, :]
                    nc.vector.tensor_scalar(e_c[:, :, :], g, 0.0, 2.0, ALU.is_ge, ALU.mult).then_inc(dve_step, 1)
                    nc.vector.scalar_tensor_tensor(out=c_t[:, :, :], in0=g, scalar=-1.0, in1=g, op0=ALU.mult, op1=ALU.max).then_inc(dve_step, 1)
                    step += 2
                    dve.wait_ge(dve_step, step)
                    nc.vector.tensor_scalar(c_t[:, :, :], c_t[:, :, :], 0.25, None, ALU.max).then_inc(dve_step, 1)
                    step += 1
                    dve.wait_ge(dve_step, step)
                    nc.vector.scalar_tensor_tensor(out=g, in0=e_c[:, :, :], scalar=-1.0, in1=c_t[:, :, :],
                                                   op0=ALU.add, op1=ALU.mult).then_inc(mod_final, 1)
                    dve.wait_ge(mod_final, 1)
                s2 = mod[:, 4 * KB:5 * KB, :]
                nc.vector.tensor_scalar(s2, s2, 1.0, None, ALU.add).then_inc(mod_final, 1)

            @block.tensor
            def _(pe):
                def mod_piece(buf, b, landed, done):
                    pe.wait_ge(stage_in[b], landed)
                    if not isinstance(done, int) or done:
                        pe.wait_ge(mod_out, done)
                    w = buf.rearrange("p (k n) -> p k n", n=MOD_COLS)
                    for m in range(MOD_BLKS):
                        for k in range(KB):
                            ins = nc.tensor.matmul(mod_ps[:, m * B:(m + 1) * B], w[:, k, m * P:(m + 1) * P], silu[:, k, :],
                                                   start=k == 0, stop=k == KB - 1)
                    ins.then_inc(mod_mm, 1)

                pe.sem_inc(acc_done, 1)
                pe.sem_inc(tp_done, 1)
                pe.wait_ge(silu_done, 1)
                pe.wait_ge(ident_done, 1)
                for pi in range(first_mod):
                    buf, b, cnt = staged(pi)
                    mod_piece(buf, b, 16 * cnt, pi)
                with pe.Fori(0, B * NCH) as n:
                    for k in range(KB):
                        if k >= 2:
                            pe.wait_ge(h_hi, n * KB + (k - 1))
                        for a in range(TT):
                            if k == 0:
                                pe.wait_ge(xhat_done, n * TT + (a + 1))
                            ins = nc.tensor.transpose(tp[:, k % 2, a * P:(a + 1) * P], x[:, a, k * P:(k + 1) * P], ident[:, :])
                        ins.then_inc(tp_done, 1)
                    pe.wait_ge(wlo_done, NW)
                    for m in range(RU):
                        w, c0 = (wq, m * P) if m < QB else (wk, (m - QB) * P)
                        pe.wait_ge(acc_free, n * UNITS + max(m - 2, 1))
                        for k in range(KB):
                            if m == 0:
                                pe.wait_ge(h_lo, n * KB + (k + 1))
                            for ws, hs in ((0, 0), (0, 1), (1, 0)):
                                ins = nc.tensor.matmul(acc[:, m % 4, :], w[:, ws, k, c0:c0 + P], hT[:, hs, k, :],
                                                       start=(k, ws, hs) == (0, 0, 0), stop=(k, ws) == (KB - 1, 1))
                        ins.then_inc(acc_done, 1)
                    for a in range(TT):
                        u = RU + a
                        pe.wait_ge(acc_free, n * UNITS + (u - 2))
                        for k in range(KB):
                            for hs, ws in ((0, 0), (0, 1), (1, 0)):
                                ins = nc.tensor.matmul(acc[:, u % 4, 0:KV], hT[:, hs, k, a * P:(a + 1) * P], wv[:, ws, k, :],
                                                       start=(k, ws, hs) == (0, 0, 0), stop=(k, hs) == (KB - 1, 1))
                        ins.then_inc(acc_done, 1)
                    for u in range(in_loop):
                        mod_piece(stage[:, u, :], u, n * 16 + 16 * (uses(u) + 1), n * in_loop + (first_mod + u))


LEAD = 18
MAX_PER_STEP = G
STEPS = [(j, k) for j in range(NCH) for k in range(TT * (j + 1))]
NS = len(STEPS)
MAXIMA = [(j, r, s, h) for j in range(NCH) for r in range(TT) for s in range(j + 1) for h in range(G)]
NM = len(MAXIMA)
assert NM == MAX_PER_STEP * NS


PAIRS = [s for s, (j, k) in enumerate(STEPS) if j and k % 2 == 0 and k < TT * j + 2]
PAIR_OF = {s + i: q for q, s in enumerate(PAIRS) for i in range(2)}
PAIR_PRODUCT = [s + 3 for s in PAIRS]
NPAIR = len(PAIRS)


def first_column(s):
    j, k = STEPS[s]
    return max(k - TT * j, 0) * P


def first_step(j):
    return sum(TT * (i + 1) for i in range(j))


def den_parts(s):
    parts = []
    if s in PAIR_PRODUCT:
        parts.append(("sum", first_column(s - 2), CH))
    if s not in PAIR_OF:
        parts.append(("own", first_column(s), CH))
    elif s in PAIRS and first_column(s + 1):
        parts.append(("own", 0, first_column(s + 1)))
    return parts


def step_plan(s, last):
    ahead, t = divmod(s + LEAD, NS)
    units = [] if ahead and last else [(ahead, MAX_PER_STEP * t + u) for u in range(MAX_PER_STEP)]
    due = shift_due(ahead, t)
    return units, None if last and due and due[0] else due


def shift_due(ahead, t):
    if t == 0:
        return (ahead - 1, NCH - 1)
    j = STEPS[t][0]
    return (ahead, j - 1) if STEPS[t - 1][0] != j else None


def attend(nc, io, scratch):
    QS, KS, VS, OS = (scratch[k] for k in ("q", "k", "v", "o"))
    PB = 8
    PIECES = 4
    PW = CH // PIECES
    with ExitStack() as ctx:
        def sb(name, shape, dt=F32):
            return ctx.enter_context(nc.sbuf_tensor(name, shape, dt))

        def sem(name):
            return ctx.enter_context(nc.semaphore(name))

        qst = [sb(f"qst{i}", [P, G, T], F32R) for i in range(2)]
        kst = [sb(f"kst{i}", [P, T], F32R) for i in range(2)]
        v = [sb(f"v{i}", [P, NT, D]) for i in range(2)]
        ones = sb("ones", [P, D])
        pair_sum = sb("pair_sum", [P, 2, G, CH])
        probs = sb("probs", [P, PB, G, CH])
        ident = sb("ident_a", [P, P])
        ident_b = sb("ident_b", [P, P], BF16)
        mask_q = sb("mask_q", [P, P], BF16)
        mask_k = sb("mask_k", [P, P], BF16)
        maxp = sb("maxp", [P, 2, TT, G, NCH])
        shift = sb("shift", [P, TT, G])
        shift2 = sb("shift2", [P, TT, P], F32R)
        den = sb("den", [P, CH])
        rden = sb("rden", [P, CH])
        o_raw = sb("o_raw", [P, CH])
        o = sb("o", [P, CH])
        ohl = sb("ohl", [P, 2, 2, CH], F32R)
        s_max = ctx.enter_context(nc.psum_tensor("s_max", [P, G, CH], F32))
        s_exp = ctx.enter_context(nc.psum_tensor("s_exp", [P, 2, CH], F32))
        o_ps = ctx.enter_context(nc.psum_tensor("o_ps", [P, CH], F32))
        den_ps = ctx.enter_context(nc.psum_tensor("den_ps", [P, CH], F32))

        const_set = sem("const_set")
        const_done = sem("const_done")
        ones_done = sem("ones_done")
        loaded = [sem(f"loaded{i}") for i in range(2)]
        max_scores = sem("max_scores")
        max_taken = [sem(f"max_taken{i}") for i in range(2)]
        shift_step = sem("shift_step")
        shift_ready = sem("shift_ready")
        shift_turned = sem("shift_turned")
        shift_in_act = sem("shift_in_act")
        shift_in_dve = sem("shift_in_dve")
        exp_scores = sem("exp_scores")
        exp_done = sem("exp_done")
        pv_done = sem("pv_done")
        pair_done = sem("pair_done")
        den_read = sem("den_read")
        o_read = sem("o_read")
        rden_done = sem("rden_done")
        o_done = sem("o_done")
        o_hi = sem("o_hi")
        o_lo = sem("o_lo")
        o_stored = [sem(f"o_stored{i}") for i in range(2)]
        NLOAD = 7

        def group_pairs(eng, body):
            with eng.Fori(0, NG // 2 - 1) as i:
                for par in range(2):
                    body(i * 2 + par, par, False)
            for par in range(2):
                body(NG - 2 + par, par, par == 1)

        with nc.Block() as block:
            @block.sync
            def _(sp):
                def load(g, par):
                    for row, part in ((0, 0), (1, 1), (2, 0)):
                        sp.dma_start(f32(qst[par][row * D:(row + 1) * D, :, :]),
                                     QS[part, bass.ds(g * P, P), :].rearrange("(h d) t -> d h t", d=D)).then_inc(loaded[par], 16)
                    for row, part in ((0, 0), (1, 0), (2, 1)):
                        sp.dma_start(f32(kst[par][row * D:(row + 1) * D, :]), KS[part, bass.ds(g * D, D), :]).then_inc(loaded[par], 16)
                    sp.dma_start(v[par][:, :, :], VS[bass.ds(g, 1), :, :, :].rearrange("g p a d -> p (g a) d")).then_inc(loaded[par], 16)

                def body(g, par, last):
                    for j in range(NCH):
                        if j == NCH - 1 and not isinstance(g, int):
                            wait_alone(sp, pv_done, g * NS + (NS + PB), (const_set, 4))
                            load(g + 2, par)
                        wait_alone(sp, o_lo, g * NCH + (j + 3), (const_set, 4))
                        sp.dma_start(OS[:, bass.ds(g * P, P), j * CH:(j + 1) * CH].rearrange("s r t -> r s t"),
                                     f32(ohl[:, j % 2, :, :])).then_inc(o_stored[j % 2], 16)

                for i, s in enumerate(o_stored):
                    sp.sem_inc(s, 16 * (i + 1))
                for par in range(2):
                    load(par, par)
                group_pairs(sp, body)
                for i, s in enumerate(o_stored):
                    sp.wait_ge(s, 16 * (NG * NCH // 2 + i + 1))

            @block.gpsimd
            def _(pool):
                for t, fill in ((ident[:, :], 0.0), (ident_b[:, :], 0.0), (mask_q[:, :], 0.0), (mask_k[:, :], 0.0)):
                    nc.gpsimd.memset(t, fill).then_inc(const_set, 1)
                nc.gpsimd.memset(ones[:, :], 1.0).then_inc(const_done, 1)
                nc.gpsimd.memset(f32(shift2[:, :, :]), 0.0).then_inc(const_done, 1)
                pool.wait_ge(const_set, 4)
                for t in (ident, ident_b):
                    nc.gpsimd.affine_select(out=t[:, :], in_=t[:, :], compare_op=ALU.not_equal, fill=1.0,
                                            base=0, pattern=[[-1, P]], channel_multiplier=1).then_inc(const_done, 1)
                nc.gpsimd.affine_select(out=mask_q[:, :], in_=mask_q[:, :], compare_op=ALU.is_ge, fill=MASKED,
                                        base=0, pattern=[[-1, P]], channel_multiplier=1).then_inc(const_done, 1)
                nc.gpsimd.affine_select(out=mask_k[:, :], in_=mask_k[:, :], compare_op=ALU.is_ge, fill=MASKED,
                                        base=0, pattern=[[1, P]], channel_multiplier=-1).then_inc(const_done, 1)

                def add_pair(g, q):
                    s, b = PAIRS[q], q % 2
                    c0 = first_column(s + 1)
                    pool.wait_ge(exp_done, g * (G * NS) + (G * (s + 2) + 2))
                    pool.wait_ge(pv_done, g * NS + (PAIR_PRODUCT[q - 2] - (0 if q >= 2 else NS) + 1 + PB))
                    nc.gpsimd.tensor_tensor(pair_sum[:, b, :, c0:CH], probs[:, s % PB, :, c0:CH], probs[:, (s + 1) % PB, :, c0:CH],
                                            ALU.add).then_inc(pair_done, 1)

                def output(g, j):
                    n, b = g * NCH + j, (j + 1) % 2
                    pool.wait_ge(rden_done, n + 2)
                    pool.wait_ge(o_read, n + 2)
                    pool.wait_ge(o_lo, n + 1)
                    nc.gpsimd.tensor_tensor(o[:, :], o_raw[:, :], rden[:, :], ALU.mult).then_inc(o_done, 1)
                    wait_alone(pool, o_done, n + 2, (const_set, 4))
                    wait_alone(pool, o_stored[b], (g * (NCH // 2) + (j // 2 + 1)) * 16, (const_set, 4))
                    nc.gpsimd.tensor_copy(ohl[:, b, 0, :], o[:, :]).then_inc(o_hi, 1)
                    pool.wait_ge(o_hi, n + 1)
                    nc.gpsimd.tensor_tensor(ohl[:, b, 1, :], o[:, :], f32(ohl[:, b, 0, :]), ALU.subtract).then_inc(o_lo, 1)

                def body(g, par, last):
                    for j in range(NCH):
                        if j == 0:
                            output(g, j)
                        for q, s in enumerate(PAIRS):
                            if STEPS[s][0] == j:
                                add_pair(g, q)
                                if STEPS[s][1] == TT:
                                    output(g, j)

                for done in (rden_done, o_read, o_lo, o_done, den_read):
                    pool.sem_inc(done, 1)
                pool.sem_inc(pair_done, PB // 2)
                group_pairs(pool, body)
                output(NG, 0)

            def turned_shift(eng_copy, eng, done, g, par, j, heads):
                eng.wait_ge(shift_turned, g * NCH + (j + 1))
                for h in heads:
                    ins = eng_copy(qst[par][3 * D:3 * D + 2, h, j * CH:(j + 1) * CH], s_max[h * D:h * D + 2, G - 1, :])
                ins.then_inc(done, 1)

            @block.scalar
            def _(act):
                def copy(dst, src):
                    return nc.scalar.activation(dst, src, ACT.Copy)

                def read_den(g, j):
                    act.wait_ge(pv_done, g * NS + (first_step(j) + PB))
                    act.wait_ge(rden_done, g * NCH + (j + 1))
                    nc.scalar.activation(den[:, :], den_ps[:, :], ACT.Copy).then_inc(den_read, 1)

                def body(g, par, last):
                    for s, (j, k) in enumerate(STEPS):
                        c0 = first_column(s)
                        _, due = step_plan(s, last)
                        for h in range(G):
                            act.wait_ge(exp_scores, g * (G * NS) + (G * s + h + 1))
                            if h == 0:
                                act.wait_ge(pv_done, g * NS + (s + 1))
                                q = PAIR_OF.get((s - PB) % NS)
                                if q is not None:
                                    act.wait_ge(pair_done, g * NPAIR + (q + 1 + PB // 2 - (0 if s >= PB else NPAIR)))
                            nc.scalar.activation(probs[:, s % PB, h, c0:CH], s_exp[:, h % 2, c0:CH], ACT.Exp,
                                                 scale=SCALE).then_inc(exp_done, 1)
                            if h == 1 and due:
                                turned_shift(copy, act, shift_in_act, g + due[0], (par + due[0]) % 2, due[1], (0, 1))
                        if k == 0:
                            read_den(g, j)

                act.sem_inc(exp_done, 2)
                for t in range(1, LEAD):
                    if due := shift_due(0, t):
                        turned_shift(copy, act, shift_in_act, 0, 0, due[1], (0, 1))
                group_pairs(act, body)
                read_den(NG, 0)

            @block.vector
            def _(dve):
                def maximum(g, m):
                    j, r, s, h = MAXIMA[m]
                    n = CH if s < j else (r + 1) * P
                    dve.wait_ge(max_scores, g * NM + (m + 1))
                    nc.vector.tensor_reduce(maxp[:, j % 2, r, h, s:s + 1], s_max[:, h, 0:n], AX.X, ALU.max).then_inc(max_taken[h % 2], 1)

                def finish_shift(g, m):
                    j = MAXIMA[m][0]
                    for taken in max_taken:
                        dve.wait_ge(taken, g * (NM // 2) + (m + 1) // 2)
                    if not isinstance(g, int) or g * NCH + j:
                        dve.wait_ge(shift_turned, g * NCH + j)
                    nc.vector.tensor_reduce(shift[:, :, :], maxp[:, j % 2, :, :, 0:j + 1], AX.X, ALU.max, negate=True).then_inc(shift_step, 1)
                    dve.wait_ge(shift_step, g * (2 * NCH) + (2 * j + 1))
                    parts = shift2[:, :, :].rearrange("p r (h d) -> p r h d", d=D)
                    nc.vector.tensor_copy(parts[:, :, :, 0], shift[:, :, :]).then_inc(shift_step, 1)
                    dve.wait_ge(shift_step, g * (2 * NCH) + (2 * j + 2))
                    nc.vector.tensor_tensor(parts[:, :, :, 1], shift[:, :, :], f32(parts[:, :, :, 0]), ALU.subtract).then_inc(shift_ready, 1)

                def copy(dst, src):
                    return nc.vector.tensor_copy(dst, src)

                def read_output(g, j):
                    dve.wait_ge(pv_done, g * NS + (first_step(j) + PB))
                    dve.wait_ge(o_done, g * NCH + (j + 1))
                    nc.vector.tensor_copy(o_raw[:, :], o_ps[:, :]).then_inc(o_read, 1)

                def invert(g, j, i):
                    if i == 0:
                        dve.wait_ge(den_read, g * NCH + (j + 2))
                        dve.wait_ge(o_done, g * NCH + (j + 1))
                    cols = slice(i * PW, (i + 1) * PW)
                    ins = nc.vector.reciprocal(rden[:, cols], den[:, cols])
                    if i == PIECES - 1:
                        ins.then_inc(rden_done, 1)

                def ahead(g, par, units, due, pieces=()):
                    for i, (a, m) in enumerate(units):
                        if i == G - 1 and due:
                            turned_shift(copy, dve, shift_in_dve, g + due[0], (par + due[0]) % 2, due[1], (2, 3))
                        maximum(g + a, m)
                        if m == NM - 1 or MAXIMA[m + 1][0] != MAXIMA[m][0]:
                            finish_shift(g + a, m)
                        if i == 1 and pieces:
                            invert(*pieces[0])
                    for piece in pieces[1 if units else 0:]:
                        invert(*piece)
                    if due and not units:
                        turned_shift(copy, dve, shift_in_dve, g + due[0], (par + due[0]) % 2, due[1], (2, 3))

                def body(g, par, last):
                    for s, (j, k) in enumerate(STEPS):
                        units, due = step_plan(s, last)
                        pieces = [(g, j, i) for i in range(PIECES) if ((1, 3, 4, 5) if j else (1, 2, 3, 3))[i] == k]
                        ahead(g, par, units, due, pieces)
                        if k == 0:
                            read_output(g, j)

                for par in range(2):
                    nc.vector.memset(f32(kst[par][3 * D:3 * D + 2, :]), 1.0).then_inc(ones_done, 1)
                dve.wait_ge(const_done, 6)
                for t in range(LEAD):
                    ahead(0, 0, [(0, MAX_PER_STEP * t + u) for u in range(MAX_PER_STEP)], shift_due(0, t) if t else None)
                group_pairs(dve, body)
                read_output(NG, 0)
                for i in range(PIECES):
                    invert(NG, 0, i)

            @block.tensor
            def _(pe):
                def max_unit(g, par, m):
                    j, r, s, h = MAXIMA[m]
                    n = CH if s < j else (r + 1) * P
                    q0 = j * CH + r * P
                    if not isinstance(g, int) or g * NM + m >= G:
                        pe.wait_ge(max_taken[h % 2], g * (NM // 2) + (m // 2 - 1))
                    ins = nc.tensor.matmul(s_max[:, h, 0:n], qst[par][0:3 * D, h, q0:q0 + P],
                                           kst[par][0:3 * D, s * CH:s * CH + n], start=True, stop=s < j)
                    if s == j:
                        ins = nc.tensor.matmul(s_max[:, h, n - P:n], ident_b[:, :], mask_q[:, :], start=False, stop=True)
                    ins.then_inc(max_scores, 1)

                def turn_shift(g, j):
                    pe.wait_ge(shift_ready, g * NCH + (j + 1))
                    for r in range(TT):
                        ins = nc.tensor.transpose(s_max[:, G - 1, r * P:(r + 1) * P], f32(shift2[:, r, :]), ident[:, :])
                    ins.then_inc(shift_turned, 1)

                def shift_read(g, j):
                    pe.wait_ge(shift_in_act, g * NCH + (j + 1))
                    pe.wait_ge(shift_in_dve, g * NCH + (j + 1))

                def head_scores(g, par, s, h):
                    j, k = STEPS[s]
                    c0 = first_column(s)
                    diag = k >= TT * j
                    pe.wait_ge(exp_done, g * (G * NS) + (G * s + h + 1))
                    ins = nc.tensor.matmul(s_exp[:, h % 2, c0:CH], kst[par][0:3 * D + 2, k * P:(k + 1) * P],
                                           qst[par][0:3 * D + 2, h, j * CH + c0:(j + 1) * CH], start=True, stop=not diag)
                    if diag:
                        ins = nc.tensor.matmul(s_exp[:, h % 2, c0:c0 + P], ident_b[:, :], mask_k[:, :], start=False, stop=True)
                    ins.then_inc(exp_scores, 1)

                def products(g, par, s):
                    j, k = STEPS[s]
                    c0 = first_column(s)
                    pe.wait_ge(exp_done, g * (G * NS) + (G * (s + 1) + 2))
                    if k == 0:
                        pe.wait_ge(o_read, g * NCH + (j + 2))
                    for h in range(G):
                        ins = nc.tensor.matmul(o_ps[h * D:(h + 1) * D, c0:CH], v[par][:, k, :], probs[:, s % PB, h, c0:CH],
                                               start=k == 0, stop=k == TT * (j + 1) - 1)
                    if not den_parts(s):
                        ins.then_inc(pv_done, 1)

                def denominators(g, par, s):
                    j, k = STEPS[s]
                    parts = den_parts(s)
                    for i, (src, lo, hi) in enumerate(parts):
                        if src == "sum":
                            q = PAIR_PRODUCT.index(s)
                            src = pair_sum[:, q % 2, :, :]
                            pe.wait_ge(pair_done, g * NPAIR + (q + 1 + PB // 2))
                        else:
                            src = probs[:, s % PB, :, :]
                        first = i == 0 and k == (3 if j else 0)
                        final = i == len(parts) - 1
                        if first:
                            pe.wait_ge(den_read, g * NCH + (j + 2))
                        for h in range(G):
                            ins = nc.tensor.matmul(den_ps[h * D:(h + 1) * D, lo:hi], ones[:, :], src[:, h, lo:hi],
                                                   start=first, stop=final and k == TT * (j + 1) - 1)
                        if final:
                            ins.then_inc(pv_done, 1)

                def body(g, par, last):
                    for s in range(NS):
                        units, due = step_plan(s, last)
                        if units and units[0] == (1, 0):
                            pe.wait_ge(loaded[1 - par], load_count(g, par))
                        for h in range(G):
                            if h == 2:
                                if s:
                                    products(g, par, s - 1)
                                if due:
                                    turn_shift(g + due[0], due[1])
                            head_scores(g, par, s, h)
                            for a, m in units[h:h + 1] if not due or h < G - 1 else ():
                                max_unit(g + a, (par + a) % 2, m)
                        if s:
                            denominators(g, par, s - 1)
                        if due:
                            shift_read(g + due[0], due[1])
                            for a, m in units[G - 1:]:
                                max_unit(g + a, (par + a) % 2, m)
                    products(g, par, NS - 1)
                    denominators(g, par, NS - 1)

                def load_count(g, par):
                    if isinstance(g, int):
                        return 16 * NLOAD * ((g + 1) // 2 + 1)
                    return (g - par) * (8 * NLOAD) + 16 * NLOAD * (1 + par)

                pe.wait_ge(const_done, 6)
                pe.wait_ge(ones_done, 2)
                pe.wait_ge(loaded[0], 16 * NLOAD)
                pe.sem_inc(pv_done, PB - 1)
                for bank in (o_ps, den_ps):
                    for h in range(G):
                        for c in range(0, CH, P):
                            ins = nc.tensor.matmul(bank[h * D:(h + 1) * D, c:c + P], ones[:, :], ident[:, :], start=True, stop=True)
                ins.then_inc(pv_done, 1)
                for t in range(LEAD):
                    due = shift_due(0, t) if t else None
                    for u in range(MAX_PER_STEP):
                        if due and u == G - 1:
                            turn_shift(0, due[1])
                            shift_read(0, due[1])
                        max_unit(0, 0, MAX_PER_STEP * t + u)
                group_pairs(pe, body)


def feed(nc, io, scratch, mod, out):
    OS, GATES = scratch["o"], scratch["gates"]
    NSTAGE = 3
    with ExitStack() as ctx:
        def sb(name, shape, dt=F32):
            return ctx.enter_context(nc.sbuf_tensor(name, shape, dt))

        def psum(name, shape):
            return ctx.enter_context(nc.psum_tensor(name, shape, F32))

        def sem(name):
            return ctx.enter_context(nc.semaphore(name))

        wo = sb("wo", [P, 2, KB, C], F32R)
        w = sb("w", [P, 2, KB, C + XW], F32R)
        bb = sb("bb", [RMAX + 1, C])
        gate_b = sb("gate_b", [P, NR])
        gates = sb("gates", [P, 2, C])
        work = sb("work", [P, NSTAGE, C])
        xh, t2, hf = (work[:, i, :] for i in range(3))
        ot = [sb(f"ot{i}", [P, 2, KB, P], F32R) for i in range(2)]
        x = [sb(f"x{i}", [P, C]) for i in range(2)]
        hT = sb("hT2", [P, 2, KB, P], F32R)
        ident = sb("ident_g", [P, P])
        stats = sb("stats2", [P, 2, 6])
        mv = sb("mv2", [P, 2])
        var = sb("var2", [P, 1])
        rstd = sb("rstd2", [P, 1])
        minus_half = sb("minus_half2", [P, 1])
        lg = sb("lg", [P, NR])
        nmax = sb("nmax", [P, 1])
        e = sb("e", [P, NR])
        esum = sb("esum", [P, 1])
        rsum = sb("rsum", [P, 1])
        pr = sb("pr", [P, NR])
        pmax = sb("pmax", [P, 1])
        rpmax = sb("rpmax", [P, 1])
        wt = sb("wt", [P, 1])
        beyond = sb("beyond", [P, NR])
        zm = sb("zm", [P, RMAX + 1])
        zt = sb("zt", [RMAX + 1, P])
        y1 = psum("y1", [P, 2, CH])
        y2 = psum("y2", [P, 2, CH])
        tp = psum("tp2", [P, 2, CH])
        z = psum("z", [P, CH])
        ztp = psum("ztp", [P, CH])

        stage_in = [sem(f"fstage_in{b}") for b in range(NSTAGE)]
        consts_in = sem("fconsts_in")
        ident_zero = sem("fident_zero")
        consts_done = sem("fconsts_done")
        whi_done = sem("fwhi_done")
        wlo_done = sem("fwlo_done")
        gates_in = sem("gates_in")
        ot_in = [sem(f"ot_in{i}") for i in range(2)]
        x_in = [sem(f"fx_in{i}") for i in range(2)]
        y1_done = sem("y1_done")
        y1_read = sem("y1_read")
        step_x = sem("step_x")
        var_done = sem("fvar_done")
        rstd_done = sem("frstd_done")
        xhat_done = sem("fxhat_done")
        tp_done = sem("ftp_done")
        hf_done = sem("hf_done")
        h_hi = sem("fh_hi")
        h_lo = sem("fh_lo")
        z_done = sem("z_done")
        main_done = sem("main_done")
        step_z = sem("step_z")
        lg_done = sem("lg_done")
        e_done = sem("e_done")
        zm_done = sem("zm_done")
        ztp_done = sem("ztp_done")
        zt_done = sem("zt_done")
        y2_done = sem("y2_done")
        t2_done = sem("t2_done")
        out_done = sem("out_done")
        stored = sem("stored")

        pieces = [(rows(io["wo"])[:, k, :], wo[:, :, k, :]) for k in range(KB)]
        pieces += [(rows(io["wT"])[:, k, :], w[:, :, k, 0:C]) for k in range(KB)]
        NP = len(pieces) + 1
        extra = work[:, (NP - 1) % NSTAGE, 0:KB * XW].rearrange("p (k n) -> p k n", n=XW)

        def split_pieces():
            for i in range(NP):
                b = i % NSTAGE
                if i < NP - 1:
                    dst = pieces[i][1]
                    yield work[:, b, :], dst[:, 0, :], dst[:, 1, :], b, i // NSTAGE + 1
                else:
                    yield extra, w[:, 0, :, C:C + XW], w[:, 1, :, C:C + XW], b, i // NSTAGE + 1

        def tiles(eng, body):
            for n in range(2):
                body(n, n)
            with eng.Fori(1, NT // 2 - 1) as i:
                for par in range(2):
                    body(i * 2 + par, par)
            for n in range(NT - 2, NT):
                body(n, n % 2)

        def is_last(n):
            return isinstance(n, int) and n == NT - 1

        def is_first(n):
            return isinstance(n, int) and n == 0

        with nc.Block() as block:
            @block.sync
            def _(sp):
                for i, (src, _) in enumerate(pieces):
                    if i >= NSTAGE:
                        sp.wait_ge(wlo_done, i - NSTAGE + 1)
                    sp.dma_start(work[:, i % NSTAGE, :], src).then_inc(stage_in[i % NSTAGE], 16)
                sp.wait_ge(wlo_done, NP - NSTAGE)
                sp.dma_start(extra[:, :, 0:RMAX], rows(io["aT"])).then_inc(consts_in, 16)
                sp.dma_start(extra[:, :, RMAX:XW], rows(io["gate_wT"])).then_inc(consts_in, 16)
                sp.dma_start(bb[0:RMAX, :], io["bT"]).then_inc(consts_in, 16)
                sp.dma_start(bb[RMAX:RMAX + 1, :], io["b"].rearrange("(a n) -> a n", a=1)).then_inc(consts_in, 16)
                sp.dma_start(gate_b[:, :], io["gate_b"].rearrange("(a n) -> a n", a=1).broadcast_to((P, NR))).then_inc(consts_in, 16)
                sp.sem_inc(stored, 16)

                def load_o(b, n, par):
                    cols = bass.ds(n * P, P)
                    for s in range(2):
                        sp.dma_start(f32(ot[par][:, s, :, :]),
                                     OS[s, bass.ds(b * C, C), cols].rearrange("(k p) t -> p k t", p=P)).then_inc(ot_in[par], 16)

                def load_x(b, n, par):
                    sp.dma_start(x[par][:, :], io["x"][bass.ds(b * T + n * P, P), :]).then_inc(x_in[par], 16)

                def store(b, n, par):
                    wait_alone(sp, out_done, b * NT + (n + 1), (consts_done, 2))
                    sp.dma_start(out[bass.ds(b * T + n * P, P), :], x[par][:, :]).then_inc(stored, 16)
                    wait_alone(sp, stored, (b * NT + n) * 16 + 32, (consts_done, 2))

                with sp.Fori(0, B) as b:
                    for i in range(2):
                        sp.dma_start(gates[:, i, :], GATES[bass.ds(b, 1), i, :].broadcast_to((P, C))).then_inc(gates_in, 16)
                    load_o(b, 0, 0)
                    load_o(b, 1, 1)
                    load_x(b, 0, 0)

                    def body(n, par):
                        if not (isinstance(n, int) and n + 2 >= NT):
                            wait_alone(sp, y1_done, b * NT + (n + 1), (consts_done, 2))
                            load_o(b, n + 2, par)
                        if not is_first(n):
                            store(b, n - 1, 1 - par)
                        if not is_last(n):
                            load_x(b, n + 1, 1 - par)

                    tiles(sp, body)
                    store(b, NT - 1, (NT - 1) % 2)

            @block.gpsimd
            def _(pool):
                nc.gpsimd.memset(ident[:, :], 0.0).then_inc(ident_zero, 1)
                nc.gpsimd.memset(minus_half[:, :], -0.5).then_inc(ident_zero, 1)
                nc.gpsimd.memset(zm[:, RMAX:RMAX + 1], 1.0).then_inc(consts_done, 1)
                pool.wait_ge(ident_zero, 2)
                nc.gpsimd.affine_select(out=ident[:, :], in_=ident[:, :], compare_op=ALU.not_equal, fill=1.0,
                                        base=0, pattern=[[-1, P]], channel_multiplier=1).then_inc(consts_done, 1)

                with pool.Fori(0, B * NT) as n:
                    pool.wait_ge(var_done, n + 1)
                    nc.gpsimd.tensor_tensor(rstd[:, :], var[:, :], minus_half[:, :], ALU.pow).then_inc(rstd_done, 1)

            @block.scalar
            def _(act):
                for i, (src, hi, _, b, cnt) in enumerate(split_pieces()):
                    if i < NP - 1:
                        act.wait_ge(stage_in[b], 16 * cnt)
                    else:
                        act.wait_ge(consts_in, 16 * 5)
                    nc.scalar.activation(hi, src, ACT.Copy).then_inc(whi_done, 1)

                with act.Fori(0, B) as b:
                    def affine(n):
                        if not is_first(n):
                            act.wait_ge(main_done, b * NT + n)
                        wait_alone(act, tp_done, b * NT + (n + 1), (whi_done, NP))
                        for k in range(KB):
                            shift, scale = (mod[:, v * KB + k, bass.ds(b, 1)] for v in (3, 4))
                            ins = nc.scalar.activation(hf[:, k * P:(k + 1) * P], tp[:, k // TT, (k % TT) * P:(k % TT + 1) * P],
                                                       ACT.Identity, bias=shift, scale=scale)
                        ins.then_inc(hf_done, 1)
                        act.wait_ge(hf_done, b * NT + (n + 1))
                        nc.scalar.activation(hT[:, 0, :, :], hf.rearrange("p (k t) -> p k t", t=P), ACT.Copy).then_inc(h_hi, 1)

                    def body(n, par):
                        act.wait_ge(lg_done, b * NT + (n + 1))
                        nc.scalar.activation(e[:, :], lg[:, :], ACT.Exp, bias=nmax[:, :], accum_out=esum[:, :]).then_inc(e_done, 1)
                        act.wait_ge(ztp_done, b * NT + (n + 1))
                        nc.scalar.activation(zt[:, :], ztp[0:RMAX + 1, 0:P], ACT.Copy).then_inc(zt_done, 1)
                        if not is_last(n):
                            affine(n + 1)

                    affine(0)
                    tiles(act, body)

            @block.vector
            def _(dve):
                for i, (src, hi, lo, _, _) in enumerate(split_pieces()):
                    dve.wait_ge(whi_done, i + 1)
                    nc.vector.tensor_tensor(lo, src, f32(hi), ALU.subtract).then_inc(wlo_done, 1)
                dve.wait_ge(wlo_done, NP)
                dve.wait_ge(consts_done, 2)

                with dve.Fori(0, B) as b:
                    dve.wait_ge(gates_in, b * 32 + 32)

                    XS = 4

                    def norm(n, par):
                        def step(ins, i):
                            ins.then_inc(step_x, 1)
                            dve.wait_ge(step_x, (b * NT + n) * XS + (i + 1))

                        dve.wait_ge(y1_done, b * NT + (n + 1))
                        if not is_first(n):
                            dve.wait_ge(tp_done, b * NT + n)
                        dve.wait_ge(x_in[par], (b * NT + n - par) * 8 + 16)
                        step(nc.vector.tensor_tensor(xh, y1[:, :, :].rearrange("p h c -> p (h c)"), gates[:, 0, :], ALU.mult), 0)
                        step(nc.vector.tensor_tensor(x[par][:, :], x[par][:, :], xh, ALU.add), 1)
                        for half in range(2):
                            ins = nc.vector.bn_stats(stats[:, half, :], x[par][:, half * CH:(half + 1) * CH])
                        ins.then_inc(step_x, 1)
                        wait_alone(dve, step_x, (b * NT + n) * XS + 3, (wlo_done, NP))
                        step(nc.vector.bn_aggr(mv[:, :], stats[:, :, :].rearrange("p h s -> p (h s)")), 3)
                        nc.vector.tensor_scalar(var[:, :], mv[:, 1:2], EPS, None, ALU.add).then_inc(var_done, 1)
                        dve.wait_ge(rstd_done, b * NT + (n + 1))
                        nc.vector.tensor_scalar(xh, x[par][:, :], mv[:, 0:1], rstd[:, :], ALU.subtract, ALU.mult).then_inc(xhat_done, 1)

                    def low_part(n):
                        dve.wait_ge(h_hi, b * NT + (n + 1))
                        nc.vector.tensor_tensor(hT[:, 1, :, :], hf.rearrange("p (k t) -> p k t", t=P), f32(hT[:, 0, :, :]),
                                                ALU.subtract).then_inc(h_lo, 1)

                    ZS = 7

                    def route(n):
                        def step(ins, i):
                            ins.then_inc(step_z, 1)
                            dve.wait_ge(step_z, (b * NT + n) * ZS + (i + 1))

                        dve.wait_ge(z_done, b * NT + (n + 1))
                        step(nc.vector.tensor_tensor(lg[:, :], z[:, RMAX:XW], gate_b[:, :], ALU.add), 0)
                        nc.vector.tensor_reduce(nmax[:, :], lg[:, :], AX.X, ALU.max, negate=True).then_inc(lg_done, 1)
                        dve.wait_ge(e_done, b * NT + (n + 1))
                        step(nc.vector.reciprocal(rsum[:, :], esum[:, :]), 1)
                        step(nc.vector.tensor_scalar(pr[:, :], e[:, :], rsum[:, :], None, ALU.mult), 2)
                        step(nc.vector.tensor_reduce(pmax[:, :], pr[:, :], AX.X, ALU.max), 3)
                        nc.vector.reciprocal(rpmax[:, :], pmax[:, :])
                        step(nc.vector.tensor_scalar(beyond[:, :], pr[:, :], pmax[:, :], None, ALU.is_lt), 4)
                        nc.vector.tensor_tensor(wt[:, :], pmax[:, :], rpmax[:, :], ALU.mult)
                        step(nc.vector.tensor_tensor(beyond[:, 1:2], beyond[:, 1:2], beyond[:, 0:1], ALU.mult), 5)
                        step(nc.vector.tensor_tensor(beyond[:, 2:3], beyond[:, 2:3], beyond[:, 1:2], ALU.mult), 6)
                        if not is_first(n):
                            dve.wait_ge(ztp_done, b * NT + n)
                        nc.vector.tensor_scalar(zm[:, 0:RANKS[0]], z[:, 0:RANKS[0]], wt[:, :], None, ALU.mult)
                        for i in range(NR - 1):
                            lo, hi = RANKS[i], RANKS[i + 1]
                            ins = nc.vector.tensor_scalar(zm[:, lo:hi], z[:, lo:hi], wt[:, :], beyond[:, i:i + 1], ALU.mult, ALU.mult)
                        ins.then_inc(zm_done, 1)

                    def finish(n, par):
                        dve.wait_ge(y2_done, b * NT + (n + 1))
                        nc.vector.tensor_tensor(t2, y2[:, :, :].rearrange("p h c -> p (h c)"), gates[:, 1, :], ALU.mult).then_inc(t2_done, 1)
                        dve.wait_ge(t2_done, b * NT + (n + 1))
                        nc.vector.tensor_tensor(x[par][:, :], x[par][:, :], t2, ALU.add).then_inc(out_done, 1)

                    def body(n, par):
                        if not is_last(n):
                            norm(n + 1, 1 - par)
                        route(n)
                        if not is_last(n):
                            low_part(n + 1)
                        finish(n, par)

                    norm(0, 0)
                    low_part(0)
                    tiles(dve, body)

            @block.tensor
            def _(pe):
                pe.wait_ge(wlo_done, NP)
                pe.wait_ge(consts_done, 2)
                with pe.Fori(0, B) as b:
                    def attention_out(n, par):
                        pe.wait_ge(ot_in[par], (b * NT + n - par) * 16 + 32)
                        if not is_first(n):
                            pe.wait_ge(xhat_done, b * NT + n)
                        for c in range(2):
                            for k in range(KB):
                                for o_s, w_s in ((0, 0), (0, 1), (1, 0)):
                                    ins = nc.tensor.matmul(y1[:, c, :], ot[par][:, o_s, k, :], wo[:, w_s, k, c * CH:(c + 1) * CH],
                                                           start=(k, o_s, w_s) == (0, 0, 0), stop=(k, o_s) == (KB - 1, 1))
                        ins.then_inc(y1_done, 1)

                    def turn(n):
                        pe.wait_ge(xhat_done, b * NT + (n + 1))
                        if not is_first(n):
                            pe.wait_ge(hf_done, b * NT + n)
                        for k in range(KB):
                            ins = nc.tensor.transpose(tp[:, k // TT, (k % TT) * P:(k % TT + 1) * P], xh[:, k * P:(k + 1) * P], ident[:, :])
                        ins.then_inc(tp_done, 1)

                    def linear(n):
                        pe.wait_ge(h_lo, b * NT + (n + 1))
                        if not is_first(n):
                            pe.wait_ge(zm_done, b * NT + n)
                        for dst, c0, c1 in ((z[:, 0:XW], C, C + XW), (y2[:, 0, :], 0, CH), (y2[:, 1, :], CH, C)):
                            if c0 == 0 and not is_first(n):
                                pe.wait_ge(t2_done, b * NT + n)
                            for k in range(KB):
                                for hs, ws in ((0, 0), (0, 1), (1, 0)):
                                    ins = nc.tensor.matmul(dst, hT[:, hs, k, :], w[:, ws, k, c0:c1], start=(k, hs, ws) == (0, 0, 0),
                                                           stop=c0 == C and (k, hs) == (KB - 1, 1))
                            if c0 == C:
                                ins.then_inc(z_done, 1)
                        ins.then_inc(main_done, 1)

                    def lora_turn(n):
                        pe.wait_ge(zm_done, b * NT + (n + 1))
                        if not is_first(n):
                            pe.wait_ge(zt_done, b * NT + n)
                        nc.tensor.transpose(ztp[0:RMAX + 1, 0:P], zm[:, :], ident[:, :]).then_inc(ztp_done, 1)

                    def lora(n):
                        pe.wait_ge(zt_done, b * NT + (n + 1))
                        for c in range(2):
                            ins = nc.tensor.matmul(y2[:, c, :], zt[:, :], bb[:, c * CH:(c + 1) * CH], start=False, stop=True)
                        ins.then_inc(y2_done, 1)

                    def body(n, par):
                        if not is_last(n):
                            attention_out(n + 1, 1 - par)
                        linear(n)
                        lora_turn(n)
                        if not is_last(n):
                            turn(n + 1)
                        lora(n)

                    attention_out(0, 0)
                    turn(0)
                    tiles(pe, body)


def build(nc, io, out):
    with ExitStack() as ctx:
        scratch = {
            "q": nc.dram_tensor("q_scratch", (2, B * C, T), F32, kind="Internal").ap(),
            "k": nc.dram_tensor("k_scratch", (2, B * KV, T), F32, kind="Internal").ap(),
            "v": nc.dram_tensor("v_scratch", (NG, P, NT, D), F32, kind="Internal").ap(),
            "o": nc.dram_tensor("o_scratch", (2, B * C, T), F32, kind="Internal").ap(),
            "gates": nc.dram_tensor("gates_scratch", (B, 2, C), F32, kind="Internal").ap(),
        }
        mod = ctx.enter_context(nc.sbuf_tensor("mod", [P, 6 * KB, B], F32))
        project(nc, io, scratch, mod)
        attend(nc, io, scratch)
        feed(nc, io, scratch, mod, out)


def rope_table():
    half = D // 2
    inv_freq = (np.float32(1.0) / np.float32(10000.0) ** (np.arange(half, dtype=np.float32) / np.float32(half))).astype(np.float32)
    ang = inv_freq[:, None] * np.arange(T, dtype=np.float32)[None, :]
    cos, sin = np.cos(ang), np.sin(ang)
    head = np.stack([np.concatenate([cos, cos]), np.concatenate([-sin, sin])], axis=1)
    return np.ascontiguousarray(np.tile(head, (P // D, 1, B)).astype(np.float32))


def kernel(L0_attn_X, L0_attn_Wq, L0_attn_Wk, L0_attn_Wv, L0_attn_Wo, L0_ffn_W, L0_ffn_b, L0_ffn_A, L0_ffn_B,
           L0_ffn_gate_w, L0_ffn_gate_b, L0_c, L0_wmod):
    import concourse.bacc as bacc
    from concourse.bass_utils import run_bass_kernel_spmd

    t = np.ascontiguousarray
    arrays = {
        "x": t(np.asarray(L0_attn_X).reshape(B * T, C)), "wq": t(L0_attn_Wq), "wk": t(L0_attn_Wk), "wv": t(L0_attn_Wv),
        "wo": t(L0_attn_Wo), "wT": t(np.asarray(L0_ffn_W).T), "b": t(L0_ffn_b), "aT": t(np.asarray(L0_ffn_A).T),
        "bT": t(np.asarray(L0_ffn_B).T), "gate_wT": t(np.asarray(L0_ffn_gate_w).T), "gate_b": t(L0_ffn_gate_b),
        "cT": t(np.asarray(L0_c).T), "wmod": t(L0_wmod), "rope": rope_table(),
    }
    nc = bacc.Bacc("TRN2", target_bir_lowering=False, num_devices=1)
    io = {k: nc.dram_tensor(f"in_{k}", a.shape, mybir.dt.from_np(a.dtype), kind="ExternalInput").ap() for k, a in arrays.items()}
    out = nc.dram_tensor("out", (B * T, C), F32, kind="ExternalOutput").ap()
    build(nc, io, out)
    r = run_bass_kernel_spmd(nc, [{f"in_{k}": a for k, a in arrays.items()}], core_ids=[0])
    return r.results[0]["out"].reshape(B, T, C)
```

```python
from contextlib import ExitStack

import numpy as np

import concourse.bass as bass
from concourse import mybir

F32 = mybir.dt.float32
F32R = mybir.dt.float32r
BF16 = mybir.dt.bfloat16
ALU = mybir.AluOpType
ACT = mybir.ActivationFunctionType
AX = mybir.AxisListType

P = 128
B, T, C = 2, 2048, 1024
H, HKV, D = 32, 8, 32
G = H // HKV
KB = C // P
CH = 512
NCH = T // CH
TT = CH // P
NT = T // P
KV = HKV * D
NG = B * HKV
RANKS = (8, 16, 32, 64)
RMAX = RANKS[-1]
NR = len(RANKS)
XW = RMAX + NR
EPS = 1e-5
MASKED = -1e30
SCALE = float(D) ** -0.5
SWAP = [(i + D // 2) % D for i in range(D)]

MOD_COLS = 256
PIECE = KB * MOD_COLS
MOD_BLKS = MOD_COLS // P


def wait_alone(eng, sem, value, met):
    if not isinstance(value, int):
        value = eng.to_reg(value)
    eng.wait_ge(*met)
    eng.wait_ge(sem, value)


def f32(ap):
    return ap.bitcast(F32)


def rows(ap, k=KB):
    return ap.rearrange("(k p) n -> p k n", p=P)


def project(nc, io, scratch, mod):
    QS, KS, VS, GATES = scratch["q"], scratch["k"], scratch["v"], scratch["gates"]
    NSTAGE = 3
    first_mod = 2 * C // MOD_COLS
    in_loop = (6 * C // MOD_COLS - first_mod) // (B * NCH)
    QB, KVB = C // P, KV // P
    UNITS = QB + KVB + TT
    RU = QB + KVB
    V_ORDER = (2, 3, 0, 1)
    LN_AFTER = 5
    with ExitStack() as ctx:
        def sb(name, shape, dt=F32):
            return ctx.enter_context(nc.sbuf_tensor(name, shape, dt))

        def sem(name):
            return ctx.enter_context(nc.semaphore(name))

        stage = sb("stage", [P, NSTAGE, PIECE])
        wq = sb("wq", [P, 2, KB, C], F32R)
        wk = sb("wk", [P, 2, KB, KV], F32R)
        wv = sb("wv", [P, 2, KB, KV], F32R)
        ident = sb("ident_f", [P, P])
        c_t = sb("c_t", [P, KB, B])
        e_c = sb("e_c", [P, KB, B])
        silu = sb("silu", [P, KB, D])
        pick = sb("pick", [P, B])
        mod_row = sb("mod_row", [P, 2, MOD_COLS])
        x = sb("x", [P, TT, C])
        stats = sb("stats", [P, TT, 2, 6])
        mv = sb("mv", [P, TT, 2])
        var = sb("var", [P, TT])
        rstd = sb("rstd", [P, TT])
        minus_half = sb("minus_half", [P, TT])
        hf = sb("hf", [P, 2, CH])
        hT = sb("hT", [P, 2, KB, CH], F32R)
        rope = sb("rope", [P, 2, CH])
        swp = sb("swp", [P, CH])
        xsin = sb("xsin", [P, CH])
        xcos = sb("xcos", [P, CH])
        q = sb("q", [P, 2, CH])
        qhl = sb("qhl", [P, 2, 2, CH], F32R)
        vt = sb("vt", [P, 2, KV])
        acc = ctx.enter_context(nc.psum_tensor("acc", [P, 4, CH], F32))
        tp = ctx.enter_context(nc.psum_tensor("tp", [P, 2, CH], F32))
        mod_ps = ctx.enter_context(nc.psum_tensor("mod_ps", [P, MOD_COLS], F32))
        mod_col = ctx.enter_context(nc.psum_tensor("mod_col", [P, MOD_BLKS, B], F32))

        consts_in = sem("consts_in")
        stage_in = [sem(f"stage_in{b}") for b in range(NSTAGE)]
        whi_done = sem("whi_done")
        wlo_done = sem("wlo_done")
        c_exp = sem("c_exp")
        silu_done = sem("silu_done")
        silu_zero = sem("silu_zero")
        mod_mm = sem("mod_mm")
        mod_row_out = sem("mod_row_out")
        mod_turned = sem("mod_turned")
        mod_out = sem("mod_out")
        mod_final = sem("mod_final")
        gates_out = sem("gates_out")
        x_in = sem("x_in")
        rope_in = sem("rope_in")
        var_done = sem("var_done")
        rstd_done = sem("rstd_done")
        xhat_done = sem("xhat_done")
        tp_done = sem("tp_done")
        h_hi = sem("h_hi")
        h_lo = sem("h_lo")
        acc_done = sem("acc_done")
        acc_free = sem("acc_free")
        v_step = sem("v_step")
        q_done = sem("q_done")
        q_hi = sem("q_hi")
        q_lo = sem("q_lo")
        q_stored = [sem(f"q_stored{b}") for b in range(2)]
        v_stored = [sem(f"v_stored{b}") for b in range(2)]
        dve_step = sem("dve_step")
        ident_zero = sem("ident_zero")
        pick_step = sem("pick_step")
        ident_done = sem("ident_done")

        wmod = rows(io["wmod"])
        pieces = [(wmod[:, :, m * MOD_COLS:(m + 1) * MOD_COLS], None) for m in range(first_mod)]
        kq = PIECE // C
        for k0 in range(0, KB, kq):
            pieces.append((rows(io["wq"])[:, k0:k0 + kq, :], (wq, k0, kq)))
        pieces.append((rows(io["wk"]), (wk, 0, KB)))
        pieces.append((rows(io["wv"]), (wv, 0, KB)))
        NP = len(pieces)
        NW = NP - first_mod

        def uses(b, before=NP):
            return len(range(b, before, NSTAGE))

        def staged(pi):
            b = pi % NSTAGE
            return stage[:, b, :], b, uses(b, pi) + 1

        def chunks(eng, body):
            with eng.Fori(0, B * NCH - 1) as n:
                body(n, False)
            body(B * NCH - 1, True)

        with nc.Block() as block:
            @block.sync
            def _(sp):
                sp.dma_start(c_t[:, :, :], io["cT"].rearrange("(k p) b -> p k b", p=P)).then_inc(consts_in, 16)
                for s in (*q_stored, *v_stored):
                    sp.sem_inc(s, 16)

                def load_x(n):
                    sp.dma_start(x[:, :, :], io["x"][bass.ds(n * CH, CH), :].rearrange("(a p) c -> p a c", p=P)).then_inc(x_in, 16)

                load_x(0)
                for pi, (src, _) in enumerate(pieces):
                    buf, b, n = staged(pi)
                    if pi >= NSTAGE:
                        before = pi - NSTAGE
                        if before < first_mod:
                            sp.wait_ge(mod_mm, before + 1)
                        else:
                            sp.wait_ge(wlo_done, before - first_mod + 1)
                    sp.dma_start(buf.rearrange("p (k n) -> p k n", n=src.shape[-1]), src).then_inc(stage_in[b], 16)
                sp.wait_ge(wlo_done, NW)

                def chunk(n, last):
                    bi, j = n // NCH, n % NCH

                    def wait(semaphore, value):
                        wait_alone(sp, semaphore, value, (wlo_done, NW))

                    wait(q_done, n * RU + 1)
                    sp.dma_start(rope[:, :, :], io["rope"][:, :, bass.ds(n * CH, CH)]).then_inc(rope_in, 16)
                    if not last:
                        wait(tp_done, n * KB + KB)
                        load_x(n + 1)
                    for u in range(in_loop):
                        wait(mod_mm, n * in_loop + (first_mod - in_loop + u + 1))
                        sp.dma_start(stage[:, u, :].rearrange("p (k n) -> p k n", n=MOD_COLS),
                                     wmod[:, :, bass.ds((n * in_loop + (first_mod + u)) * MOD_COLS, MOD_COLS)]).then_inc(stage_in[u], 16)
                    for m in range(RU):
                        wait(q_lo, n * RU + (m + 3))
                        if m < QB:
                            dst = QS[:, bass.ds(bi * C + m * P, P), bass.ds(j * CH, CH)]
                        else:
                            dst = KS[:, bass.ds(bi * KV + (m - QB) * P, P), bass.ds(j * CH, CH)]
                        sp.dma_start(dst.rearrange("s r t -> r s t"), f32(qhl[:, m % 2, :, :])).then_inc(q_stored[m % 2], 16)
                    for i, a in enumerate(V_ORDER):
                        wait(acc_free, n * UNITS + (RU + i + 5))
                        sp.dma_start(VS[bass.ds(bi * HKV, HKV), :, bass.ds(j * TT + a, 1), :].rearrange("g p a d -> p g (a d)"),
                                     vt[:, a % 2, :].rearrange("p (g d) -> p g d", d=D)).then_inc(v_stored[a % 2], 16)

                chunks(sp, chunk)
                sp.wait_ge(mod_final, 3)
                for gi, first in enumerate((2 * KB, 5 * KB)):
                    for b in range(B):
                        sp.dma_start(GATES[b, gi, :].rearrange("(k p) -> p k", p=P),
                                     mod[:, first:first + KB, b], allow_slow_non_contiguous=True).then_inc(gates_out, 16)
                sp.wait_ge(gates_out, 16 * 2 * B)
                for s in q_stored:
                    sp.wait_ge(s, 16 * (B * NCH * RU // 2 + 1))
                for s in v_stored:
                    sp.wait_ge(s, 16 * (B * NCH * TT // 2 + 1))

            @block.gpsimd
            def _(pool):
                nc.gpsimd.memset(ident[:, :], 0.0).then_inc(ident_zero, 1)
                nc.gpsimd.memset(minus_half[:, :], -0.5).then_inc(ident_zero, 1)
                nc.gpsimd.memset(silu[:, :, :], 0.0).then_inc(silu_zero, 1)
                nc.gpsimd.memset(pick[:, :], 0.0).then_inc(pick_step, 1)
                for c in range(P // D):
                    pool.wait_ge(pick_step, c + 1)
                    nc.gpsimd.affine_select(out=pick[:, :], in_=pick[:, :], compare_op=ALU.not_equal, fill=1.0,
                                            base=-c * D, pattern=[[-1, B]], channel_multiplier=1).then_inc(pick_step, 1)
                pool.wait_ge(ident_zero, 2)
                nc.gpsimd.affine_select(out=ident[:, :], in_=ident[:, :], compare_op=ALU.not_equal, fill=1.0,
                                        base=0, pattern=[[-1, P]], channel_multiplier=1).then_inc(ident_done, 1)
                pool.sem_inc(q_lo, 2)

                def root(n):
                    pool.wait_ge(var_done, n + 1)
                    nc.gpsimd.tensor_tensor(rstd[:, :], var[:, :], minus_half[:, :], ALU.pow).then_inc(rstd_done, 1)

                def chunk(n, last):
                    for m in range(RU):
                        if m == LN_AFTER and not last:
                            root(n + 1)
                        pool.wait_ge(q_hi, n * RU + (m + 1))
                        pool.wait_ge(q_stored[m % 2], (n * (RU // 2) + (m // 2 + 1)) * 16)
                        nc.gpsimd.tensor_tensor(qhl[:, m % 2, 1, :], q[:, m % 2, :], f32(qhl[:, m % 2, 0, :]),
                                                ALU.subtract).then_inc(q_lo, 1)

                root(0)
                chunks(pool, chunk)

            @block.scalar
            def _(act):
                act.wait_ge(consts_in, 16)
                nc.scalar.activation(e_c[:, :, :], c_t[:, :, :], ACT.Exp, scale=-1.0).then_inc(c_exp, 1)

                def modulate(n):
                    for k in range(KB):
                        if k >= 2:
                            act.wait_ge(h_lo, n * KB + (k - 1))
                        if not isinstance(n, int):
                            if k < KB - 1:
                                act.wait_ge(v_step, n * (KB - 1) + (k + 2 - KB))
                            else:
                                act.wait_ge(acc_done, n * UNITS)
                        wait_alone(act, tp_done, n * KB + (k + 1), (mod_out, first_mod))
                        shift, scale = (mod[:, v * KB + k, bass.ds(n // NCH, 1)] for v in (0, 1))
                        nc.scalar.activation(hf[:, k % 2, :], tp[:, k % 2, :], ACT.Identity, bias=shift, scale=scale)
                        nc.scalar.activation(hT[:, 0, k, :], tp[:, k % 2, :], ACT.Identity, bias=shift, scale=scale).then_inc(h_hi, 1)

                def chunk(n, last):
                    for m in range(RU):
                        act.wait_ge(q_done, n * RU + (m + 2))
                        act.wait_ge(q_stored[m % 2], (n * (RU // 2) + (m // 2 + 1)) * 16)
                        nc.scalar.activation(qhl[:, m % 2, 0, :], q[:, m % 2, :], ACT.Copy).then_inc(q_hi, 1)
                    if not last:
                        modulate(n + 1)

                modulate(0)
                for pi, (src, w) in enumerate(pieces):
                    if w:
                        buf, b, cnt = staged(pi)
                        act.wait_ge(stage_in[b], 16 * cnt)
                        nc.scalar.activation(w[0][:, 0, w[1]:w[1] + w[2], :], buf.rearrange("p (k n) -> p k n", n=src.shape[-1]),
                                             ACT.Copy).then_inc(whi_done, 1)
                chunks(act, chunk)

            @block.vector
            def _(dve):
                dve.sem_inc(acc_free, 4)
                dve.sem_inc(q_done, 1)
                dve.wait_ge(c_exp, 1)
                nc.vector.tensor_scalar(e_c[:, :, :], e_c[:, :, :], 1.0, None, ALU.add).then_inc(dve_step, 1)
                dve.wait_ge(dve_step, 1)
                nc.vector.reciprocal(e_c[:, :, :], e_c[:, :, :]).then_inc(dve_step, 1)
                dve.wait_ge(dve_step, 2)
                dve.wait_ge(silu_zero, 1)
                nc.vector.tensor_tensor(silu[:, :, 0:B], e_c[:, :, :], c_t[:, :, :], ALU.mult).then_inc(silu_done, 1)

                def read_mod_row(u, piece):
                    dve.wait_ge(mod_mm, piece + 1)
                    if not isinstance(piece, int) or piece >= 2:
                        dve.wait_ge(mod_turned, piece - 1)
                    nc.vector.tensor_copy(mod_row[:, u, :], mod_ps[:, :]).then_inc(mod_row_out, 1)

                STEPS = 2 + 2 * RU

                def norm(n, base, step):
                    dve.wait_ge(x_in, n * 16 + 16)
                    for a in range(TT):
                        for half in range(2):
                            ins = nc.vector.bn_stats(stats[:, a, half, :], x[:, a, half * CH:(half + 1) * CH])
                    ins.then_inc(dve_step, 1)
                    wait_alone(dve, dve_step, base + (step + 1), (silu_done, 1))
                    for a in range(TT):
                        ins = nc.vector.bn_aggr(mv[:, a, :], stats[:, a, :, :].rearrange("p h s -> p (h s)"))
                    ins.then_inc(dve_step, 1)
                    dve.wait_ge(dve_step, base + (step + 2))
                    nc.vector.tensor_scalar(var[:, :], mv[:, :, 1], EPS, None, ALU.add).then_inc(var_done, 1)
                    dve.wait_ge(rstd_done, n + 1)
                    for a in range(TT):
                        nc.vector.tensor_scalar(x[:, a, :], x[:, a, :], mv[:, a, 0:1], rstd[:, a:a + 1],
                                                ALU.subtract, ALU.mult).then_inc(xhat_done, 1)

                def low_parts(n, blocks):
                    for k in blocks:
                        dve.wait_ge(h_hi, n * KB + (k + 1))
                        nc.vector.tensor_tensor(hT[:, 1, k, :], hf[:, k % 2, :], f32(hT[:, 0, k, :]), ALU.subtract).then_inc(h_lo, 1)

                def chunk(n, last):
                    base, step = n * STEPS, 4
                    dve.wait_ge(rope_in, n * 16 + 16)
                    for m in range(RU):
                        if m == RU - 1:
                            read_mod_row(0, n * in_loop + first_mod)
                        if m == LN_AFTER and not last:
                            norm(n + 1, base, step)
                            step += 2
                        summed = n * RU + (m + 1)
                        if not isinstance(n, int):
                            summed = dve.to_reg(summed)
                        wait_alone(dve, acc_done, n * UNITS + (m + 1), (silu_done, 1))
                        dve.wait_ge(q_done, summed)
                        nc.vector.stream_shuffle(swp[:, :], acc[:, m % 4, :], SWAP).then_inc(dve_step, 1)
                        nc.vector.tensor_tensor(xcos[:, :], acc[:, m % 4, :], rope[:, 0, :], ALU.mult).then_inc(acc_free, 1)
                        step += 1
                        dve.wait_ge(dve_step, base + step)
                        nc.vector.tensor_tensor(xsin[:, :], swp[:, :], rope[:, 1, :], ALU.mult).then_inc(dve_step, 1)
                        step += 1
                        dve.wait_ge(dve_step, base + step)
                        dve.wait_ge(acc_free, n * UNITS + (m + 5))
                        dve.wait_ge(q_lo, n * RU + (m + 1))
                        nc.vector.tensor_tensor(q[:, m % 2, :], xcos[:, :], xsin[:, :], ALU.add).then_inc(q_done, 1)
                    read_mod_row(1, n * in_loop + (first_mod + 1))
                    for u in range(in_loop):
                        dve.wait_ge(mod_turned, n * in_loop + (first_mod + u + 1))
                        nc.vector.tensor_copy(mod[:, bass.ds((n * in_loop + (first_mod + u)) * MOD_BLKS, MOD_BLKS), :],
                                              mod_col[:, :, :]).then_inc(mod_out, 1)
                    if not last:
                        low_parts(n + 1, range(KB - 2))
                    for i, a in enumerate(V_ORDER):
                        dve.wait_ge(acc_done, n * UNITS + (RU + i + 1))
                        dve.wait_ge(v_stored[a % 2], (n * (TT // 2) + (i // 2 + 1)) * 16)
                        nc.vector.tensor_copy(vt[:, a % 2, :], acc[:, (RU + a) % 4, 0:KV]).then_inc(acc_free, 1)
                    if not last:
                        low_parts(n + 1, range(KB - 2, KB))

                norm(0, 0, 2)
                for pi in range(first_mod + 1):
                    if pi < first_mod:
                        read_mod_row(pi % 2, pi)
                    if pi:
                        dve.wait_ge(mod_turned, pi)
                        one = 1.0 if (pi - 1) * MOD_COLS >= C else 0.0
                        nc.vector.tensor_scalar(mod[:, (pi - 1) * MOD_BLKS:pi * MOD_BLKS, :], mod_col[:, :, :],
                                                one, None, ALU.add).then_inc(mod_out, 1)
                low_parts(0, range(KB))
                wn = 0
                for pi, (src, w) in enumerate(pieces):
                    if w:
                        wn += 1
                        buf, b, _ = staged(pi)
                        v = buf.rearrange("p (k n) -> p k n", n=src.shape[-1])
                        dve.wait_ge(whi_done, wn)
                        nc.vector.tensor_tensor(w[0][:, 1, w[1]:w[1] + w[2], :], v, f32(w[0][:, 0, w[1]:w[1] + w[2], :]),
                                                ALU.subtract).then_inc(wlo_done, 1)
                chunks(dve, chunk)
                dve.wait_ge(mod_out, 6 * C // MOD_COLS)
                step = B * NCH * STEPS + 2
                for first in (2 * KB, 5 * KB):
                    g = mod[:, first:first + KB, :]
                    nc.vector.tensor_scalar(e_c[:, :, :], g, 0.0, 2.0, ALU.is_ge, ALU.mult).then_inc(dve_step, 1)
                    nc.vector.scalar_tensor_tensor(out=c_t[:, :, :], in0=g, scalar=-1.0, in1=g, op0=ALU.mult, op1=ALU.max).then_inc(dve_step, 1)
                    step += 2
                    dve.wait_ge(dve_step, step)
                    nc.vector.tensor_scalar(c_t[:, :, :], c_t[:, :, :], 0.25, None, ALU.max).then_inc(dve_step, 1)
                    step += 1
                    dve.wait_ge(dve_step, step)
                    nc.vector.scalar_tensor_tensor(out=g, in0=e_c[:, :, :], scalar=-1.0, in1=c_t[:, :, :],
                                                   op0=ALU.add, op1=ALU.mult).then_inc(mod_final, 1)
                    dve.wait_ge(mod_final, 1)
                s2 = mod[:, 4 * KB:5 * KB, :]
                nc.vector.tensor_scalar(s2, s2, 1.0, None, ALU.add).then_inc(mod_final, 1)

            @block.tensor
            def _(pe):
                def mod_rows(buf, b, landed, piece):
                    pe.wait_ge(stage_in[b], landed)
                    if not isinstance(piece, int) or piece:
                        pe.wait_ge(mod_row_out, piece)
                    w = buf.rearrange("p (k n) -> p k n", n=MOD_COLS)
                    for k in range(KB):
                        c = k % 4 * D
                        ins = nc.tensor.matmul(mod_ps[c:c + D, :], silu[:, k, :], w[:, k, :], start=k < 4, stop=k >= KB - 4)
                    ins.then_inc(mod_mm, 1)

                def mod_turn(u, piece):
                    pe.wait_ge(mod_row_out, piece + 1)
                    if not isinstance(piece, int) or piece:
                        pe.wait_ge(mod_out, piece)
                    for m in range(MOD_BLKS):
                        ins = nc.tensor.matmul(mod_col[:, m, :], mod_row[:, u, m * P:(m + 1) * P], pick[:, :], start=True, stop=True)
                    ins.then_inc(mod_turned, 1)

                pe.wait_ge(silu_done, 1)
                pe.wait_ge(ident_done, 1)
                pe.wait_ge(pick_step, P // D + 1)
                for pi in range(first_mod + 1):
                    if pi < first_mod:
                        buf, b, cnt = staged(pi)
                        mod_rows(buf, b, 16 * cnt, pi)
                    if pi:
                        mod_turn((pi - 1) % 2, pi - 1)

                def in_rows(n, u):
                    mod_rows(stage[:, u, :], u, n * 16 + 16 * (uses(u) + 1), n * in_loop + (first_mod + u))

                def turn(n, k):
                    if k >= 2:
                        pe.wait_ge(h_hi, n * KB + (k - 1))
                    for a in range(TT):
                        if k == 0:
                            pe.wait_ge(xhat_done, n * TT + (a + 1))
                        ins = nc.tensor.transpose(tp[:, k % 2, a * P:(a + 1) * P], x[:, a, k * P:(k + 1) * P], ident[:, :])
                    ins.then_inc(tp_done, 1)

                def chunk(n, last):
                    for m in range(RU):
                        w, c0 = (wq, m * P) if m < QB else (wk, (m - QB) * P)
                        if m in (0, QB):
                            pe.wait_ge(wlo_done, NW - 2 if m == 0 else NW - 1)
                        if m == RU - 1:
                            in_rows(n, 0)
                        pe.wait_ge(acc_free, n * UNITS + (m + 1))
                        for k in range(KB):
                            if m == 0:
                                pe.wait_ge(h_lo, n * KB + (k + 1))
                            for ws, hs in ((0, 0), (0, 1), (1, 0)):
                                ins = nc.tensor.matmul(acc[:, m % 4, :], w[:, ws, k, c0:c0 + P], hT[:, hs, k, :],
                                                       start=(k, ws, hs) == (0, 0, 0), stop=(k, ws) == (KB - 1, 1))
                        ins.then_inc(acc_done, 1)
                    in_rows(n, 1)
                    pe.wait_ge(wlo_done, NW)
                    pe.wait_ge(acc_free, n * UNITS + (RU + 4))
                    for k in range(KB):
                        for a in V_ORDER:
                            for hs, ws in ((0, 0), (0, 1), (1, 0)):
                                ins = nc.tensor.matmul(acc[:, (RU + a) % 4, 0:KV], hT[:, hs, k, a * P:(a + 1) * P], wv[:, ws, k, :],
                                                       start=(k, ws, hs) == (0, 0, 0), stop=(k, hs) == (KB - 1, 1))
                            if k == KB - 1:
                                ins.then_inc(acc_done, 1)
                        if k < KB - 1:
                            ins.then_inc(v_step, 1)
                        if k < in_loop:
                            mod_turn(k, n * in_loop + (first_mod + k))
                        if not last:
                            turn(n + 1, k)

                for k in range(KB):
                    turn(0, k)
                chunks(pe, chunk)


LEAD = 18
MAX_PER_STEP = G
STEPS = [(j, k) for j in range(NCH) for k in range(TT * (j + 1))]
NS = len(STEPS)
MAXIMA = [(j, r, s, h) for j in range(NCH) for r in range(TT) for s in range(j + 1) for h in range(G)]
NM = len(MAXIMA)
assert NM == MAX_PER_STEP * NS


PAIRS = [s for s, (j, k) in enumerate(STEPS) if j and k % 2 == 0 and k < TT * j + 2]
PAIR_OF = {s + i: q for q, s in enumerate(PAIRS) for i in range(2)}
PAIR_PRODUCT = [s + 3 for s in PAIRS]
NPAIR = len(PAIRS)


def first_column(s):
    j, k = STEPS[s]
    return max(k - TT * j, 0) * P


def first_step(j):
    return sum(TT * (i + 1) for i in range(j))


def den_parts(s):
    parts = []
    if s in PAIR_PRODUCT:
        parts.append(("sum", first_column(s - 2), CH))
    if s not in PAIR_OF:
        parts.append(("own", first_column(s), CH))
    elif s in PAIRS and first_column(s + 1):
        parts.append(("own", 0, first_column(s + 1)))
    return parts


def step_plan(s, last):
    ahead, t = divmod(s + LEAD, NS)
    units = [] if ahead and last else [(ahead, MAX_PER_STEP * t + u) for u in range(MAX_PER_STEP)]
    due = shift_due(ahead, t)
    return units, None if last and due and due[0] else due


def shift_due(ahead, t):
    if t == 0:
        return (ahead - 1, NCH - 1)
    j = STEPS[t][0]
    return (ahead, j - 1) if STEPS[t - 1][0] != j else None


def attend(nc, io, scratch):
    QS, KS, VS, OS = (scratch[k] for k in ("q", "k", "v", "o"))
    PB = 8
    PIECES = 4
    PW = CH // PIECES
    with ExitStack() as ctx:
        def sb(name, shape, dt=F32):
            return ctx.enter_context(nc.sbuf_tensor(name, shape, dt))

        def sem(name):
            return ctx.enter_context(nc.semaphore(name))

        qst = [sb(f"qst{i}", [P, G, T], F32R) for i in range(2)]
        kst = [sb(f"kst{i}", [P, T], F32R) for i in range(2)]
        v = [sb(f"v{i}", [P, NT, D]) for i in range(2)]
        ones = sb("ones", [P, D])
        pair_sum = sb("pair_sum", [P, 2, G, CH])
        probs = sb("probs", [P, PB, G, CH])
        ident = sb("ident_a", [P, P])
        ident_b = sb("ident_b", [P, P], BF16)
        mask_q = sb("mask_q", [P, P], BF16)
        mask_k = sb("mask_k", [P, P], BF16)
        maxp = sb("maxp", [P, 2, TT, G, NCH])
        shift = sb("shift", [P, TT, G])
        shift2 = sb("shift2", [P, TT, P], F32R)
        den = sb("den", [P, CH])
        rden = sb("rden", [P, CH])
        o_raw = sb("o_raw", [P, CH])
        o = sb("o", [P, CH])
        ohl = sb("ohl", [P, 2, 2, CH], F32R)
        s_max = ctx.enter_context(nc.psum_tensor("s_max", [P, G, CH], F32))
        s_exp = ctx.enter_context(nc.psum_tensor("s_exp", [P, 2, CH], F32))
        o_ps = ctx.enter_context(nc.psum_tensor("o_ps", [P, CH], F32))
        den_ps = ctx.enter_context(nc.psum_tensor("den_ps", [P, CH], F32))

        const_set = sem("const_set")
        const_done = sem("const_done")
        ones_done = sem("ones_done")
        loaded = [sem(f"loaded{i}") for i in range(2)]
        first_in = [sem(f"first_in{j}") for j in range(NCH)]
        max_scores = sem("max_scores")
        max_taken = [sem(f"max_taken{i}") for i in range(2)]
        shift_step = sem("shift_step")
        shift_ready = sem("shift_ready")
        shift_turned = sem("shift_turned")
        shift_in_act = sem("shift_in_act")
        shift_in_dve = sem("shift_in_dve")
        exp_scores = sem("exp_scores")
        exp_done = sem("exp_done")
        pv_done = sem("pv_done")
        pair_done = sem("pair_done")
        den_read = sem("den_read")
        o_summed = sem("o_summed")
        o_read = sem("o_read")
        rden_done = sem("rden_done")
        o_done = sem("o_done")
        o_hi = sem("o_hi")
        o_lo = sem("o_lo")
        o_stored = [sem(f"o_stored{i}") for i in range(2)]
        NLOAD = 7
        NFIRST = 1

        def group_pairs(eng, body):
            with eng.Fori(0, NG // 2 - 1) as i:
                for par in range(2):
                    body(i * 2 + par, par, False)
            for par in range(2):
                body(NG - 2 + par, par, par == 1)

        with nc.Block() as block:
            @block.sync
            def _(sp):
                def load_by_chunks(g, par):
                    for j in range(NCH):
                        cols = slice(j * CH, (j + 1) * CH)
                        for row, part in ((0, 0), (1, 1), (2, 0)):
                            sp.dma_start(f32(qst[par][row * D:(row + 1) * D, :, cols]),
                                         QS[part, g * P:(g + 1) * P, cols].rearrange("(h d) t -> d h t", d=D)).then_inc(first_in[j], 16)
                        for row, part in ((0, 0), (1, 0), (2, 1)):
                            sp.dma_start(f32(kst[par][row * D:(row + 1) * D, cols]), KS[part, g * D:(g + 1) * D, cols]).then_inc(first_in[j], 16)
                    sp.dma_start(v[par][:, :, :], VS[g, :, :, :]).then_inc(loaded[par], 16)

                def load(g, par):
                    for row, part in ((0, 0), (1, 1), (2, 0)):
                        sp.dma_start(f32(qst[par][row * D:(row + 1) * D, :, :]),
                                     QS[part, bass.ds(g * P, P), :].rearrange("(h d) t -> d h t", d=D)).then_inc(loaded[par], 16)
                    for row, part in ((0, 0), (1, 0), (2, 1)):
                        sp.dma_start(f32(kst[par][row * D:(row + 1) * D, :]), KS[part, bass.ds(g * D, D), :]).then_inc(loaded[par], 16)
                    sp.dma_start(v[par][:, :, :], VS[bass.ds(g, 1), :, :, :].rearrange("g p a d -> p (g a) d")).then_inc(loaded[par], 16)

                def body(g, par, last):
                    for j in range(NCH):
                        if j == NCH - 1 and not isinstance(g, int):
                            wait_alone(sp, pv_done, g * NS + (NS + PB), (const_set, 4))
                            load(g + 2, par)
                        wait_alone(sp, o_lo, g * NCH + (j + 3), (const_set, 4))
                        sp.dma_start(OS[:, bass.ds(g * P, P), j * CH:(j + 1) * CH].rearrange("s r t -> r s t"),
                                     f32(ohl[:, j % 2, :, :])).then_inc(o_stored[j % 2], 16)

                for i, s in enumerate(o_stored):
                    sp.sem_inc(s, 16 * (i + 1))
                load_by_chunks(0, 0)
                load(1, 1)
                group_pairs(sp, body)
                for i, s in enumerate(o_stored):
                    sp.wait_ge(s, 16 * (NG * NCH // 2 + i + 1))

            @block.gpsimd
            def _(pool):
                for t, fill in ((ident[:, :], 0.0), (ident_b[:, :], 0.0), (mask_q[:, :], 0.0), (mask_k[:, :], 0.0)):
                    nc.gpsimd.memset(t, fill).then_inc(const_set, 1)
                nc.gpsimd.memset(ones[:, :], 1.0).then_inc(const_done, 1)
                nc.gpsimd.memset(f32(shift2[:, :, :]), 0.0).then_inc(const_done, 1)
                pool.wait_ge(const_set, 4)
                for t in (ident, ident_b):
                    nc.gpsimd.affine_select(out=t[:, :], in_=t[:, :], compare_op=ALU.not_equal, fill=1.0,
                                            base=0, pattern=[[-1, P]], channel_multiplier=1).then_inc(const_done, 1)
                nc.gpsimd.affine_select(out=mask_q[:, :], in_=mask_q[:, :], compare_op=ALU.is_ge, fill=MASKED,
                                        base=0, pattern=[[-1, P]], channel_multiplier=1).then_inc(const_done, 1)
                nc.gpsimd.affine_select(out=mask_k[:, :], in_=mask_k[:, :], compare_op=ALU.is_ge, fill=MASKED,
                                        base=0, pattern=[[1, P]], channel_multiplier=-1).then_inc(const_done, 1)

                def add_pair(g, q):
                    s, b = PAIRS[q], q % 2
                    c0 = first_column(s + 1)
                    pool.wait_ge(exp_done, g * (G * NS) + (G * (s + 2) + 2))
                    pool.wait_ge(pv_done, g * NS + (PAIR_PRODUCT[q - 2] - (0 if q >= 2 else NS) + 1 + PB))
                    nc.gpsimd.tensor_tensor(pair_sum[:, b, :, c0:CH], probs[:, s % PB, :, c0:CH], probs[:, (s + 1) % PB, :, c0:CH],
                                            ALU.add).then_inc(pair_done, 1)

                def output(g, j):
                    n, b = g * NCH + j, (j + 1) % 2
                    pool.wait_ge(rden_done, n + 2)
                    pool.wait_ge(o_read, n + 2)
                    pool.wait_ge(o_lo, n + 1)
                    nc.gpsimd.tensor_tensor(o[:, :], o_raw[:, :], rden[:, :], ALU.mult).then_inc(o_done, 1)
                    wait_alone(pool, o_done, n + 2, (const_set, 4))
                    wait_alone(pool, o_stored[b], (g * (NCH // 2) + (j // 2 + 1)) * 16, (const_set, 4))
                    nc.gpsimd.tensor_copy(ohl[:, b, 0, :], o[:, :]).then_inc(o_hi, 1)
                    pool.wait_ge(o_hi, n + 1)
                    nc.gpsimd.tensor_tensor(ohl[:, b, 1, :], o[:, :], f32(ohl[:, b, 0, :]), ALU.subtract).then_inc(o_lo, 1)

                def body(g, par, last):
                    for j in range(NCH):
                        if j == 0:
                            output(g, j)
                        for q, s in enumerate(PAIRS):
                            if STEPS[s][0] == j:
                                add_pair(g, q)
                                if STEPS[s][1] == TT:
                                    output(g, j)

                for done in (rden_done, o_read, o_lo, o_done, den_read):
                    pool.sem_inc(done, 1)
                pool.sem_inc(pair_done, PB // 2)
                group_pairs(pool, body)
                output(NG, 0)

            def turned_shift(eng_copy, eng, done, g, par, j, heads):
                eng.wait_ge(shift_turned, g * NCH + (j + 1))
                for h in heads:
                    ins = eng_copy(qst[par][3 * D:3 * D + 2, h, j * CH:(j + 1) * CH], s_max[h * D:h * D + 2, G - 1, :])
                ins.then_inc(done, 1)

            @block.scalar
            def _(act):
                def copy(dst, src):
                    return nc.scalar.activation(dst, src, ACT.Copy)

                def read_den(g, j):
                    act.wait_ge(pv_done, g * NS + (first_step(j) + PB))
                    act.wait_ge(rden_done, g * NCH + (j + 1))
                    nc.scalar.activation(den[:, :], den_ps[:, :], ACT.Copy).then_inc(den_read, 1)

                def body(g, par, last):
                    for s, (j, k) in enumerate(STEPS):
                        c0 = first_column(s)
                        _, due = step_plan(s, last)
                        for h in range(G):
                            act.wait_ge(exp_scores, g * (G * NS) + (G * s + h + 1))
                            if h == 0:
                                act.wait_ge(pv_done, g * NS + (s + 1))
                                q = PAIR_OF.get((s - PB) % NS)
                                if q is not None:
                                    act.wait_ge(pair_done, g * NPAIR + (q + 1 + PB // 2 - (0 if s >= PB else NPAIR)))
                            nc.scalar.activation(probs[:, s % PB, h, c0:CH], s_exp[:, h % 2, c0:CH], ACT.Exp,
                                                 scale=SCALE).then_inc(exp_done, 1)
                            if h == G - 1 and due:
                                turned_shift(copy, act, shift_in_act, g + due[0], (par + due[0]) % 2, due[1], (0, 1))
                        if k == 0:
                            read_den(g, j)

                act.sem_inc(exp_done, 2)
                for t in range(1, LEAD):
                    if due := shift_due(0, t):
                        turned_shift(copy, act, shift_in_act, 0, 0, due[1], (0, 1))
                group_pairs(act, body)
                read_den(NG, 0)

            @block.vector
            def _(dve):
                def maximum(g, m):
                    j, r, s, h = MAXIMA[m]
                    n = CH if s < j else (r + 1) * P
                    dve.wait_ge(max_scores, g * NM + (m + 1))
                    nc.vector.tensor_reduce(maxp[:, j % 2, r, h, s:s + 1], s_max[:, h, 0:n], AX.X, ALU.max).then_inc(max_taken[h % 2], 1)

                def finish_shift(g, m):
                    j = MAXIMA[m][0]
                    for taken in max_taken:
                        dve.wait_ge(taken, g * (NM // 2) + (m + 1) // 2)
                    if not isinstance(g, int) or g * NCH + j:
                        dve.wait_ge(shift_turned, g * NCH + j)
                    nc.vector.tensor_reduce(shift[:, :, :], maxp[:, j % 2, :, :, 0:j + 1], AX.X, ALU.max, negate=True).then_inc(shift_step, 1)
                    dve.wait_ge(shift_step, g * (2 * NCH) + (2 * j + 1))
                    parts = shift2[:, :, :].rearrange("p r (h d) -> p r h d", d=D)
                    nc.vector.tensor_copy(parts[:, :, :, 0], shift[:, :, :]).then_inc(shift_step, 1)
                    dve.wait_ge(shift_step, g * (2 * NCH) + (2 * j + 2))
                    nc.vector.tensor_tensor(parts[:, :, :, 1], shift[:, :, :], f32(parts[:, :, :, 0]), ALU.subtract).then_inc(shift_ready, 1)

                def copy(dst, src):
                    return nc.vector.tensor_copy(dst, src)

                def read_output(g, j):
                    dve.wait_ge(o_summed, g * NCH + (j + 1))
                    dve.wait_ge(o_done, g * NCH + (j + 1))
                    nc.vector.tensor_copy(o_raw[:, :], o_ps[:, :]).then_inc(o_read, 1)

                def invert(g, j, i):
                    if i == 0:
                        dve.wait_ge(den_read, g * NCH + (j + 2))
                        dve.wait_ge(o_done, g * NCH + (j + 1))
                    cols = slice(i * PW, (i + 1) * PW)
                    ins = nc.vector.reciprocal(rden[:, cols], den[:, cols])
                    if i == PIECES - 1:
                        ins.then_inc(rden_done, 1)

                def ahead(g, par, units, due, pieces=(), output=None):
                    for i, (a, m) in enumerate(units):
                        if i == G - 1 and due:
                            turned_shift(copy, dve, shift_in_dve, g + due[0], (par + due[0]) % 2, due[1], (2, 3))
                        maximum(g + a, m)
                        if m == NM - 1 or MAXIMA[m + 1][0] != MAXIMA[m][0]:
                            finish_shift(g + a, m)
                        if i == 1 and pieces:
                            invert(*pieces[0])
                        if i == 2 and output:
                            read_output(*output)
                    if output and not units:
                        read_output(*output)
                    for piece in pieces[1 if units else 0:]:
                        invert(*piece)
                    if due and not units:
                        turned_shift(copy, dve, shift_in_dve, g + due[0], (par + due[0]) % 2, due[1], (2, 3))

                def body(g, par, last):
                    for s, (j, k) in enumerate(STEPS):
                        units, due = step_plan(s, last)
                        pieces = [(g, j, i) for i in range(PIECES) if ((1, 3, 4, 5) if j else (1, 2, 3, 3))[i] == k]
                        ahead(g, par, units, due, pieces, (g, j) if k == 0 else None)

                for par in range(2):
                    nc.vector.memset(f32(kst[par][3 * D:3 * D + 2, :]), 1.0).then_inc(ones_done, 1)
                dve.wait_ge(const_done, 6)
                for t in range(LEAD):
                    ahead(0, 0, [(0, MAX_PER_STEP * t + u) for u in range(MAX_PER_STEP)], shift_due(0, t) if t else None)
                group_pairs(dve, body)
                read_output(NG, 0)
                for i in range(PIECES):
                    invert(NG, 0, i)

            @block.tensor
            def _(pe):
                def max_unit(g, par, m):
                    j, r, s, h = MAXIMA[m]
                    n = CH if s < j else (r + 1) * P
                    q0 = j * CH + r * P
                    if not isinstance(g, int) or g * NM + m >= G:
                        pe.wait_ge(max_taken[h % 2], g * (NM // 2) + (m // 2 - 1))
                    ins = nc.tensor.matmul(s_max[:, h, 0:n], qst[par][0:3 * D, h, q0:q0 + P],
                                           kst[par][0:3 * D, s * CH:s * CH + n], start=True, stop=s < j)
                    if s == j:
                        ins = nc.tensor.matmul(s_max[:, h, n - P:n], ident_b[:, :], mask_q[:, :], start=False, stop=True)
                    ins.then_inc(max_scores, 1)

                def turn_shift(g, j):
                    pe.wait_ge(shift_ready, g * NCH + (j + 1))
                    for r in range(TT):
                        ins = nc.tensor.transpose(s_max[:, G - 1, r * P:(r + 1) * P], f32(shift2[:, r, :]), ident[:, :])
                    ins.then_inc(shift_turned, 1)

                def shift_read(g, j):
                    pe.wait_ge(shift_in_act, g * NCH + (j + 1))
                    pe.wait_ge(shift_in_dve, g * NCH + (j + 1))

                def head_scores(g, par, s, h):
                    j, k = STEPS[s]
                    c0 = first_column(s)
                    diag = k >= TT * j
                    pe.wait_ge(exp_done, g * (G * NS) + (G * s + h + 1))
                    ins = nc.tensor.matmul(s_exp[:, h % 2, c0:CH], kst[par][0:3 * D + 2, k * P:(k + 1) * P],
                                           qst[par][0:3 * D + 2, h, j * CH + c0:(j + 1) * CH], start=True, stop=not diag)
                    if diag:
                        ins = nc.tensor.matmul(s_exp[:, h % 2, c0:c0 + P], ident_b[:, :], mask_k[:, :], start=False, stop=True)
                    ins.then_inc(exp_scores, 1)

                def products(g, par, s):
                    j, k = STEPS[s]
                    c0 = first_column(s)
                    pe.wait_ge(exp_done, g * (G * NS) + (G * (s + 1) + 2))
                    if k == 0:
                        pe.wait_ge(o_read, g * NCH + (j + 2))
                    for h in range(G):
                        ins = nc.tensor.matmul(o_ps[h * D:(h + 1) * D, c0:CH], v[par][:, k, :], probs[:, s % PB, h, c0:CH],
                                               start=k == 0, stop=k == TT * (j + 1) - 1)
                    if k == TT * (j + 1) - 1:
                        ins.then_inc(o_summed, 1)
                    elif not den_parts(s):
                        ins.then_inc(pv_done, 1)

                def denominators(g, par, s):
                    j, k = STEPS[s]
                    parts = den_parts(s)
                    for i, (src, lo, hi) in enumerate(parts):
                        if src == "sum":
                            q = PAIR_PRODUCT.index(s)
                            src = pair_sum[:, q % 2, :, :]
                            pe.wait_ge(pair_done, g * NPAIR + (q + 1 + PB // 2))
                        else:
                            src = probs[:, s % PB, :, :]
                        first = i == 0 and k == (3 if j else 0)
                        final = i == len(parts) - 1
                        if first:
                            pe.wait_ge(den_read, g * NCH + (j + 2))
                        for h in range(G):
                            ins = nc.tensor.matmul(den_ps[h * D:(h + 1) * D, lo:hi], ones[:, :], src[:, h, lo:hi],
                                                   start=first, stop=final and k == TT * (j + 1) - 1)
                        if final:
                            ins.then_inc(pv_done, 1)

                def body(g, par, last):
                    held = None
                    for s in range(NS):
                        units, due = step_plan(s, last)
                        if units and units[0] == (1, 0):
                            pe.wait_ge(loaded[1 - par], load_count(g, par))
                        for h in range(G):
                            if h == 2:
                                if s:
                                    products(g, par, s - 1)
                                if due:
                                    turn_shift(g + due[0], due[1])
                            head_scores(g, par, s, h)
                            if h == 0 and held:
                                shift_read(g + held[0][0], held[0][1])
                                for a, m in held[1]:
                                    max_unit(g + a, (par + a) % 2, m)
                            for a, m in units[h:h + 1] if not due or h < G - 1 else ():
                                max_unit(g + a, (par + a) % 2, m)
                        if s:
                            denominators(g, par, s - 1)
                        held = (due, units[G - 1:]) if due else None
                    products(g, par, NS - 1)
                    denominators(g, par, NS - 1)

                def load_count(g, par):
                    more = 16 * (NFIRST - NLOAD) * par
                    if isinstance(g, int):
                        return 16 * NLOAD * ((g + 1) // 2 + 1) + more
                    return (g - par) * (8 * NLOAD) + (16 * NLOAD * (1 + par) + more)

                pe.wait_ge(const_done, 6)
                pe.wait_ge(ones_done, 2)
                pe.sem_inc(pv_done, PB - 1)
                for bank, done in ((o_ps, o_summed), (den_ps, pv_done)):
                    for h in range(G):
                        for c in range(0, CH, P):
                            ins = nc.tensor.matmul(bank[h * D:(h + 1) * D, c:c + P], ones[:, :], ident[:, :], start=True, stop=True)
                    ins.then_inc(done, 1)
                for t in range(LEAD):
                    j, k = STEPS[t]
                    if k == 0:
                        pe.wait_ge(first_in[j], 16 * 6)
                    due = shift_due(0, t) if t else None
                    for u in range(MAX_PER_STEP):
                        if due and u == G - 1:
                            turn_shift(0, due[1])
                            shift_read(0, due[1])
                        max_unit(0, 0, MAX_PER_STEP * t + u)
                for landed in first_in:
                    pe.wait_ge(landed, 16 * 6)
                pe.wait_ge(loaded[0], 16 * NFIRST)
                group_pairs(pe, body)


def feed(nc, io, scratch, mod, out):
    OS, GATES = scratch["o"], scratch["gates"]
    NSTAGE = 4
    TILES = B * NT
    with ExitStack() as ctx:
        def sb(name, shape, dt=F32):
            return ctx.enter_context(nc.sbuf_tensor(name, shape, dt))

        def psum(name, shape):
            return ctx.enter_context(nc.psum_tensor(name, shape, F32))

        def sem(name):
            return ctx.enter_context(nc.semaphore(name))

        wo = sb("wo", [P, 2, KB, C], F32R)
        w = sb("w", [P, 2, KB, C + XW], F32R)
        bb = sb("bb", [RMAX + 1, C])
        gate_b = sb("gate_b", [P, NR])
        gates = sb("gates", [P, B, 2, C])
        work = sb("work", [P, NSTAGE, C])
        xh, t2, hf = (work[:, i, :] for i in range(3))
        ot = [sb(f"ot{i}", [P, 2, KB, P], F32R) for i in range(2)]
        x = [sb(f"x{i}", [P, C]) for i in range(2)]
        hT = sb("hT2", [P, 2, KB, P], F32R)
        ident = sb("ident_g", [P, P])
        stats = sb("stats2", [P, 2, 6])
        mv = sb("mv2", [P, 2])
        var = sb("var2", [P, 1])
        rstd = sb("rstd2", [P, 1])
        minus_half = sb("minus_half2", [P, 1])
        lg = sb("lg", [P, NR])
        nmax = sb("nmax", [P, 1])
        e = sb("e", [P, NR])
        esum = sb("esum", [P, 1])
        rsum = sb("rsum", [P, 1])
        pr = sb("pr", [P, NR])
        pmax = sb("pmax", [P, 1])
        rpmax = sb("rpmax", [P, 1])
        wt = sb("wt", [P, 1])
        beyond = sb("beyond", [P, NR])
        zm = sb("zm", [P, RMAX + 1])
        zt = sb("zt", [RMAX + 1, P])
        y1 = psum("y1", [P, 2, CH])
        y2 = psum("y2", [P, 2, CH])
        tp = psum("tp2", [P, 2, CH])
        z = psum("z", [P, CH])
        ztp = psum("ztp", [P, CH])

        stage_in = [sem(f"fstage_in{b}") for b in range(NSTAGE)]
        consts_in = sem("fconsts_in")
        ident_zero = sem("fident_zero")
        consts_done = sem("fconsts_done")
        whi_done = sem("fwhi_done")
        wlo_done = sem("fwlo_done")
        gates_in = sem("gates_in")
        ot_in = [sem(f"ot_in{i}") for i in range(2)]
        x_in = [sem(f"fx_in{i}") for i in range(2)]
        y1_done = sem("y1_done")
        y1_read = sem("y1_read")
        step_x = sem("step_x")
        var_done = sem("fvar_done")
        rstd_done = sem("frstd_done")
        xhat_done = sem("fxhat_done")
        tp_done = sem("ftp_done")
        hf_done = sem("hf_done")
        h_hi = sem("fh_hi")
        h_lo = sem("fh_lo")
        z_done = sem("z_done")
        main_done = sem("main_done")
        step_z = sem("step_z")
        lg_done = sem("lg_done")
        e_done = sem("e_done")
        zm_done = sem("zm_done")
        ztp_done = sem("ztp_done")
        zt_done = sem("zt_done")
        y2_done = sem("y2_done")
        t2_done = sem("t2_done")
        out_done = sem("out_done")
        stored = sem("stored")

        pieces = [(rows(io["wo"])[:, k, :], wo[:, :, k, :]) for k in range(KB)]
        pieces += [(rows(io["wT"])[:, k, :], w[:, :, k, 0:C]) for k in range(KB)]
        NP = len(pieces) + 1
        extra = work[:, (NP - 1) % NSTAGE, 0:KB * XW].rearrange("p (k n) -> p k n", n=XW)

        def split_pieces():
            for i in range(NP):
                b = i % NSTAGE
                if i < NP - 1:
                    dst = pieces[i][1]
                    yield work[:, b, :], dst[:, 0, :], dst[:, 1, :], b, i // NSTAGE + 1
                else:
                    yield extra, w[:, 0, :, C:C + XW], w[:, 1, :, C:C + XW], b, i // NSTAGE + 1

        def tiles(eng, body):
            for n in range(2):
                body(n, n)
            with eng.Fori(1, TILES // 2 - 1) as i:
                for par in range(2):
                    body(i * 2 + par, par)
            for n in range(TILES - 2, TILES):
                body(n, n % 2)

        def is_last(n):
            return isinstance(n, int) and n == TILES - 1

        def is_first(n):
            return isinstance(n, int) and n == 0

        with nc.Block() as block:
            @block.sync
            def _(sp):
                def load_o(n, par):
                    cols = bass.ds(n % NT * P, P)
                    for s in range(2):
                        sp.dma_start(f32(ot[par][:, s, :, :]),
                                     OS[s, bass.ds(n // NT * C, C), cols].rearrange("(k p) t -> p k t", p=P)).then_inc(ot_in[par], 16)

                def load_x(n, par):
                    sp.dma_start(x[par][:, :], io["x"][bass.ds(n * P, P), :]).then_inc(x_in[par], 16)

                for i, (src, _) in enumerate(pieces):
                    if i == KB:
                        load_o(0, 0)
                        load_x(0, 0)
                        load_o(1, 1)
                    if i >= NSTAGE:
                        sp.wait_ge(wlo_done, i - NSTAGE + 1)
                    sp.dma_start(work[:, i % NSTAGE, :], src).then_inc(stage_in[i % NSTAGE], 16)
                sp.wait_ge(wlo_done, NP - NSTAGE)
                sp.dma_start(extra[:, :, 0:RMAX], rows(io["aT"])).then_inc(consts_in, 16)
                sp.dma_start(extra[:, :, RMAX:XW], rows(io["gate_wT"])).then_inc(consts_in, 16)
                sp.dma_start(bb[0:RMAX, :], io["bT"]).then_inc(consts_in, 16)
                sp.dma_start(bb[RMAX:RMAX + 1, :], io["b"].rearrange("(a n) -> a n", a=1)).then_inc(consts_in, 16)
                sp.dma_start(gate_b[:, :], io["gate_b"].rearrange("(a n) -> a n", a=1).broadcast_to((P, NR))).then_inc(consts_in, 16)
                for b in range(B):
                    for i in range(2):
                        sp.dma_start(gates[:, b, i, :], GATES[b:b + 1, i, :].broadcast_to((P, C))).then_inc(gates_in, 16)
                sp.sem_inc(stored, 16)

                def store(n, par):
                    wait_alone(sp, out_done, n + 1, (consts_done, 2))
                    sp.dma_start(out[bass.ds(n * P, P), :], x[par][:, :]).then_inc(stored, 16)
                    wait_alone(sp, stored, n * 16 + 32, (consts_done, 2))

                def body(n, par):
                    if not (isinstance(n, int) and n + 2 >= TILES):
                        wait_alone(sp, y1_done, n + 1, (consts_done, 2))
                        load_o(n + 2, par)
                    if not is_first(n):
                        store(n - 1, 1 - par)
                    if not is_last(n):
                        load_x(n + 1, 1 - par)

                tiles(sp, body)
                store(TILES - 1, (TILES - 1) % 2)

            @block.gpsimd
            def _(pool):
                nc.gpsimd.memset(ident[:, :], 0.0).then_inc(ident_zero, 1)
                nc.gpsimd.memset(minus_half[:, :], -0.5).then_inc(ident_zero, 1)
                nc.gpsimd.memset(zm[:, RMAX:RMAX + 1], 1.0).then_inc(consts_done, 1)
                pool.wait_ge(ident_zero, 2)
                nc.gpsimd.affine_select(out=ident[:, :], in_=ident[:, :], compare_op=ALU.not_equal, fill=1.0,
                                        base=0, pattern=[[-1, P]], channel_multiplier=1).then_inc(consts_done, 1)

                with pool.Fori(0, TILES) as n:
                    pool.wait_ge(var_done, n + 1)
                    nc.gpsimd.tensor_tensor(rstd[:, :], var[:, :], minus_half[:, :], ALU.pow).then_inc(rstd_done, 1)

            @block.scalar
            def _(act):
                for i, (src, hi, _, b, cnt) in enumerate(split_pieces()):
                    if i < NP - 1:
                        act.wait_ge(stage_in[b], 16 * cnt)
                    else:
                        act.wait_ge(consts_in, 16 * 5)
                    nc.scalar.activation(hi, src, ACT.Copy).then_inc(whi_done, 1)

                def affine(n):
                    if not is_first(n):
                        act.wait_ge(main_done, n)
                    wait_alone(act, tp_done, n + 1, (whi_done, NP))
                    for k in range(KB):
                        shift, scale = (mod[:, v * KB + k, bass.ds(n // NT, 1)] for v in (3, 4))
                        ins = nc.scalar.activation(hf[:, k * P:(k + 1) * P], tp[:, k // TT, (k % TT) * P:(k % TT + 1) * P],
                                                   ACT.Identity, bias=shift, scale=scale)
                    ins.then_inc(hf_done, 1)
                    act.wait_ge(hf_done, n + 1)
                    nc.scalar.activation(hT[:, 0, :, :], hf.rearrange("p (k t) -> p k t", t=P), ACT.Copy).then_inc(h_hi, 1)

                def body(n, par):
                    act.wait_ge(lg_done, n + 1)
                    nc.scalar.activation(e[:, :], lg[:, :], ACT.Exp, bias=nmax[:, :], accum_out=esum[:, :]).then_inc(e_done, 1)
                    act.wait_ge(ztp_done, n + 1)
                    nc.scalar.activation(zt[:, :], ztp[0:RMAX + 1, 0:P], ACT.Copy).then_inc(zt_done, 1)
                    if not is_last(n):
                        affine(n + 1)

                affine(0)
                tiles(act, body)

            @block.vector
            def _(dve):
                for i, (src, hi, lo, _, _) in enumerate(split_pieces()):
                    dve.wait_ge(whi_done, i + 1)
                    nc.vector.tensor_tensor(lo, src, f32(hi), ALU.subtract).then_inc(wlo_done, 1)
                dve.wait_ge(wlo_done, NP)
                dve.wait_ge(consts_done, 2)

                dve.wait_ge(gates_in, 16 * 2 * B)

                XS = 4

                def norm(n, par):
                    def step(ins, i):
                        ins.then_inc(step_x, 1)
                        dve.wait_ge(step_x, n * XS + (i + 1))

                    dve.wait_ge(y1_done, n + 1)
                    if not is_first(n):
                        dve.wait_ge(tp_done, n)
                    dve.wait_ge(x_in[par], (n - par) * 8 + 16)
                    step(nc.vector.tensor_tensor(xh, y1[:, :, :].rearrange("p h c -> p (h c)"), gates[:, bass.ds(n // NT, 1), 0, :].rearrange("p b c -> p (b c)"), ALU.mult), 0)
                    step(nc.vector.tensor_tensor(x[par][:, :], x[par][:, :], xh, ALU.add), 1)
                    for half in range(2):
                        ins = nc.vector.bn_stats(stats[:, half, :], x[par][:, half * CH:(half + 1) * CH])
                    ins.then_inc(step_x, 1)
                    wait_alone(dve, step_x, n * XS + 3, (wlo_done, NP))
                    step(nc.vector.bn_aggr(mv[:, :], stats[:, :, :].rearrange("p h s -> p (h s)")), 3)
                    nc.vector.tensor_scalar(var[:, :], mv[:, 1:2], EPS, None, ALU.add).then_inc(var_done, 1)
                    dve.wait_ge(rstd_done, n + 1)
                    nc.vector.tensor_scalar(xh, x[par][:, :], mv[:, 0:1], rstd[:, :], ALU.subtract, ALU.mult).then_inc(xhat_done, 1)

                def low_part(n):
                    dve.wait_ge(h_hi, n + 1)
                    nc.vector.tensor_tensor(hT[:, 1, :, :], hf.rearrange("p (k t) -> p k t", t=P), f32(hT[:, 0, :, :]),
                                            ALU.subtract).then_inc(h_lo, 1)

                ZS = 7

                def route(n):
                    def step(ins, i):
                        ins.then_inc(step_z, 1)
                        dve.wait_ge(step_z, n * ZS + (i + 1))

                    dve.wait_ge(z_done, n + 1)
                    step(nc.vector.tensor_tensor(lg[:, :], z[:, RMAX:XW], gate_b[:, :], ALU.add), 0)
                    nc.vector.tensor_reduce(nmax[:, :], lg[:, :], AX.X, ALU.max, negate=True).then_inc(lg_done, 1)
                    dve.wait_ge(e_done, n + 1)
                    step(nc.vector.reciprocal(rsum[:, :], esum[:, :]), 1)
                    step(nc.vector.tensor_scalar(pr[:, :], e[:, :], rsum[:, :], None, ALU.mult), 2)
                    step(nc.vector.tensor_reduce(pmax[:, :], pr[:, :], AX.X, ALU.max), 3)
                    nc.vector.reciprocal(rpmax[:, :], pmax[:, :])
                    step(nc.vector.tensor_scalar(beyond[:, :], pr[:, :], pmax[:, :], None, ALU.is_lt), 4)
                    nc.vector.tensor_tensor(wt[:, :], pmax[:, :], rpmax[:, :], ALU.mult)
                    step(nc.vector.tensor_tensor(beyond[:, 1:2], beyond[:, 1:2], beyond[:, 0:1], ALU.mult), 5)
                    step(nc.vector.tensor_tensor(beyond[:, 2:3], beyond[:, 2:3], beyond[:, 1:2], ALU.mult), 6)
                    if not is_first(n):
                        dve.wait_ge(ztp_done, n)
                    nc.vector.tensor_scalar(zm[:, 0:RANKS[0]], z[:, 0:RANKS[0]], wt[:, :], None, ALU.mult)
                    for i in range(NR - 1):
                        lo, hi = RANKS[i], RANKS[i + 1]
                        ins = nc.vector.tensor_scalar(zm[:, lo:hi], z[:, lo:hi], wt[:, :], beyond[:, i:i + 1], ALU.mult, ALU.mult)
                    ins.then_inc(zm_done, 1)

                def finish(n, par):
                    dve.wait_ge(y2_done, n + 1)
                    nc.vector.tensor_tensor(t2, y2[:, :, :].rearrange("p h c -> p (h c)"), gates[:, bass.ds(n // NT, 1), 1, :].rearrange("p b c -> p (b c)"), ALU.mult).then_inc(t2_done, 1)
                    dve.wait_ge(t2_done, n + 1)
                    nc.vector.tensor_tensor(x[par][:, :], x[par][:, :], t2, ALU.add).then_inc(out_done, 1)

                def body(n, par):
                    if not is_last(n):
                        norm(n + 1, 1 - par)
                    route(n)
                    if not is_last(n):
                        low_part(n + 1)
                    finish(n, par)

                norm(0, 0)
                low_part(0)
                tiles(dve, body)

            @block.tensor
            def _(pe):
                pe.wait_ge(wlo_done, KB)
                pe.wait_ge(consts_done, 2)
                def attention_out(n, par):
                    pe.wait_ge(ot_in[par], (n - par) * 16 + 32)
                    if not is_first(n):
                        pe.wait_ge(xhat_done, n)
                    for c in range(2):
                        for k in range(KB):
                            for o_s, w_s in ((0, 0), (0, 1), (1, 0)):
                                ins = nc.tensor.matmul(y1[:, c, :], ot[par][:, o_s, k, :], wo[:, w_s, k, c * CH:(c + 1) * CH],
                                                       start=(k, o_s, w_s) == (0, 0, 0), stop=(k, o_s) == (KB - 1, 1))
                    ins.then_inc(y1_done, 1)

                def turn(n):
                    pe.wait_ge(xhat_done, n + 1)
                    if not is_first(n):
                        pe.wait_ge(hf_done, n)
                    for k in range(KB):
                        ins = nc.tensor.transpose(tp[:, k // TT, (k % TT) * P:(k % TT + 1) * P], xh[:, k * P:(k + 1) * P], ident[:, :])
                    ins.then_inc(tp_done, 1)

                def linear(n):
                    if is_first(n):
                        pe.wait_ge(wlo_done, NP)
                    pe.wait_ge(h_lo, n + 1)
                    if not is_first(n):
                        pe.wait_ge(zm_done, n)
                    for dst, c0, c1 in ((z[:, 0:XW], C, C + XW), (y2[:, 0, :], 0, CH), (y2[:, 1, :], CH, C)):
                        if c0 == 0 and not is_first(n):
                            pe.wait_ge(t2_done, n)
                        for k in range(KB):
                            for hs, ws in ((0, 0), (0, 1), (1, 0)):
                                ins = nc.tensor.matmul(dst, hT[:, hs, k, :], w[:, ws, k, c0:c1], start=(k, hs, ws) == (0, 0, 0),
                                                       stop=c0 == C and (k, hs) == (KB - 1, 1))
                        if c0 == C:
                            ins.then_inc(z_done, 1)
                    ins.then_inc(main_done, 1)

                def lora_turn(n):
                    pe.wait_ge(zm_done, n + 1)
                    if not is_first(n):
                        pe.wait_ge(zt_done, n)
                    nc.tensor.transpose(ztp[0:RMAX + 1, 0:P], zm[:, :], ident[:, :]).then_inc(ztp_done, 1)

                def lora(n):
                    pe.wait_ge(zt_done, n + 1)
                    for c in range(2):
                        ins = nc.tensor.matmul(y2[:, c, :], zt[:, :], bb[:, c * CH:(c + 1) * CH], start=False, stop=True)
                    ins.then_inc(y2_done, 1)

                def body(n, par):
                    if not is_last(n):
                        attention_out(n + 1, 1 - par)
                    linear(n)
                    lora_turn(n)
                    if not is_last(n):
                        turn(n + 1)
                    lora(n)

                attention_out(0, 0)
                turn(0)
                tiles(pe, body)


def build(nc, io, out):
    with ExitStack() as ctx:
        scratch = {
            "q": nc.dram_tensor("q_scratch", (2, B * C, T), F32, kind="Internal").ap(),
            "k": nc.dram_tensor("k_scratch", (2, B * KV, T), F32, kind="Internal").ap(),
            "v": nc.dram_tensor("v_scratch", (NG, P, NT, D), F32, kind="Internal").ap(),
            "o": nc.dram_tensor("o_scratch", (2, B * C, T), F32, kind="Internal").ap(),
            "gates": nc.dram_tensor("gates_scratch", (B, 2, C), F32, kind="Internal").ap(),
        }
        mod = ctx.enter_context(nc.sbuf_tensor("mod", [P, 6 * KB, B], F32))
        project(nc, io, scratch, mod)
        attend(nc, io, scratch)
        feed(nc, io, scratch, mod, out)


def rope_table():
    half = D // 2
    inv_freq = (np.float32(1.0) / np.float32(10000.0) ** (np.arange(half, dtype=np.float32) / np.float32(half))).astype(np.float32)
    ang = inv_freq[:, None] * np.arange(T, dtype=np.float32)[None, :]
    cos, sin = np.cos(ang), np.sin(ang)
    head = np.stack([np.concatenate([cos, cos]), np.concatenate([-sin, sin])], axis=1)
    return np.ascontiguousarray(np.tile(head, (P // D, 1, B)).astype(np.float32))


def kernel(L0_attn_X, L0_attn_Wq, L0_attn_Wk, L0_attn_Wv, L0_attn_Wo, L0_ffn_W, L0_ffn_b, L0_ffn_A, L0_ffn_B,
           L0_ffn_gate_w, L0_ffn_gate_b, L0_c, L0_wmod):
    import concourse.bacc as bacc
    from concourse.bass_utils import run_bass_kernel_spmd

    t = np.ascontiguousarray
    arrays = {
        "x": t(np.asarray(L0_attn_X).reshape(B * T, C)), "wq": t(L0_attn_Wq), "wk": t(L0_attn_Wk), "wv": t(L0_attn_Wv),
        "wo": t(L0_attn_Wo), "wT": t(np.asarray(L0_ffn_W).T), "b": t(L0_ffn_b), "aT": t(np.asarray(L0_ffn_A).T),
        "bT": t(np.asarray(L0_ffn_B).T), "gate_wT": t(np.asarray(L0_ffn_gate_w).T), "gate_b": t(L0_ffn_gate_b),
        "cT": t(np.asarray(L0_c).T), "wmod": t(L0_wmod), "rope": rope_table(),
    }
    nc = bacc.Bacc("TRN2", target_bir_lowering=False, num_devices=1)
    io = {k: nc.dram_tensor(f"in_{k}", a.shape, mybir.dt.from_np(a.dtype), kind="ExternalInput").ap() for k, a in arrays.items()}
    out = nc.dram_tensor("out", (B * T, C), F32, kind="ExternalOutput").ap()
    build(nc, io, out)
    r = run_bass_kernel_spmd(nc, [{f"in_{k}": a for k, a in arrays.items()}], core_ids=[0])
    return r.results[0]["out"].reshape(B, T, C)
```
